# Optimizing a Trainium2 kernel written in Bass

```python
import numpy as np
import jax
import jax.numpy as jnp

def _softmax(x, axis=-1):
    return jax.nn.softmax(x, axis=axis)

def _gelu(x):
    return jax.nn.gelu(x, approximate=True)

def _silu(x):
    return jax.nn.silu(x)

def _sigmoid(x):
    return jax.nn.sigmoid(x)

def _layernorm(x, axis=-1, eps=1e-05):
    m = jnp.mean(x, axis=axis, keepdims=True)
    v = jnp.var(x, axis=axis, keepdims=True)
    return (x - m) / jnp.sqrt(v + eps)

def _scatter_add(tgt, idx, src, axis=0):
    return tgt.at[idx].add(src)

def _segment_sum(src, seg, n):
    return jax.ops.segment_sum(src, seg, n)
kernel_name = 'mk_macaron_d1_jaxref_r8_9f1245'

def setup_inputs(seed: int=0):
    np.random.seed(seed)
    _w = jnp.asarray

    def _L0_attn_setup():
        import jax, jax.numpy as jnp
        import numpy as np
        NUM_HEADS = 8
        CHUNK = 64

        def _retention(q, k, v):
            B, Hn, L, DK = q.shape
            DV = v.shape[-1]
            C = CHUNK
            N = L // C
            dt = q.dtype
            gamma = (1.0 - jnp.exp2(-5.0 - jnp.arange(Hn, dtype=jnp.float32))).astype(dt)
            q = q * DK ** (-0.5)
            idx = jnp.arange(C)
            diff = idx[:, None] - idx[None, :]
            D = jnp.where(diff >= 0, gamma[:, None, None] ** diff, 0.0).astype(dt)
            decay_q = (gamma[:, None] ** (idx[None, :] + 1)).astype(dt)
            decay_k = (gamma[:, None] ** (C - 1 - idx[None, :])).astype(dt)
            decay_s = (gamma ** C).astype(dt)

            def to_chunks(x):
                return jnp.moveaxis(x.reshape(B, Hn, N, C, -1), 2, 0)
            qs, ks, vs = map(to_chunks, (q, k, v))

            def step(S, x):
                qc, kc, vc = x
                attn = jnp.einsum('bhid,bhjd->bhij', qc, kc) * D
                o_intra = jnp.einsum('bhij,bhje->bhie', attn, vc)
                o_inter = jnp.einsum('bhid,bhde->bhie', qc * decay_q[None, :, :, None], S)
                S_new = decay_s[None, :, None, None] * S + jnp.einsum('bhjd,bhje->bhde', kc * decay_k[None, :, :, None], vc)
                return (S_new, o_intra + o_inter)
            S0 = jnp.zeros((B, Hn, DK, DV), dt)
            _, o = jax.lax.scan(step, S0, (qs, ks, vs))
            return jnp.moveaxis(o, 0, 2).reshape(B, Hn, L, DV)

        def _xavier(key, fan_in, fan_out, gain=2 ** (-2.5)):
            limit = gain * np.sqrt(6.0 / (fan_in + fan_out))
            return jax.random.uniform(key, (fan_in, fan_out), jnp.float32, -limit, limit)
        key = jax.random.key(seed)
        k0, k1, k2, k3, k4 = jax.random.split(key, 5)
        B, L, D = (2, 512, 128)
        return {'hidden_states': jax.random.normal(k0, (B, L, D), jnp.float32), 'rel_pos': jnp.zeros((1,), jnp.float32), 'Wq': _xavier(k1, D, D), 'Wk': _xavier(k2, D, D), 'Wv': _xavier(k3, D, D), 'Wo': _xavier(k4, D, D)}
    _L0_attn_in = _L0_attn_setup()

    def _L0_ffn_setup():
        import jax, jax.numpy as jnp
        import numpy as np
        D_MODEL = 128
        D_FF = 512
        NUM_EXPERTS = 8
        TOP_K = 2
        BATCH = 4
        SEQ = 256
        key = jax.random.key(seed)
        ks = jax.random.split(key, 8)
        s = 0.02
        x = jax.random.normal(ks[0], (BATCH, SEQ, D_MODEL), dtype=jnp.float32)
        router_w = jax.random.normal(ks[1], (D_MODEL, NUM_EXPERTS), dtype=jnp.float32) * s
        router_b = jnp.zeros((NUM_EXPERTS,), dtype=jnp.float32)
        W1 = jax.random.normal(ks[2], (NUM_EXPERTS, D_MODEL, D_FF), dtype=jnp.float32) * s
        b1 = jnp.zeros((NUM_EXPERTS, D_FF), dtype=jnp.float32)
        W2 = jax.random.normal(ks[3], (NUM_EXPERTS, D_FF, D_MODEL), dtype=jnp.float32) * s
        b2 = jnp.zeros((NUM_EXPERTS, D_MODEL), dtype=jnp.float32)
        return {'x': x, 'router_w': router_w, 'router_b': router_b, 'W1': W1, 'b1': b1, 'W2': W2, 'b2': b2}
    _L0_ffn_in = _L0_ffn_setup()
    _d = {'L0_attn_hidden_states': _L0_attn_in['hidden_states'], 'L0_attn_rel_pos': _L0_attn_in['rel_pos'], 'L0_attn_Wq': _L0_attn_in['Wq'], 'L0_attn_Wk': _L0_attn_in['Wk'], 'L0_attn_Wv': _L0_attn_in['Wv'], 'L0_attn_Wo': _L0_attn_in['Wo'], 'L0_ffn_router_w': _L0_ffn_in['router_w'], 'L0_ffn_router_b': _L0_ffn_in['router_b'], 'L0_ffn_W1': _L0_ffn_in['W1'], 'L0_ffn_b1': _L0_ffn_in['b1'], 'L0_ffn_W2': _L0_ffn_in['W2'], 'L0_ffn_b2': _L0_ffn_in['b2']}
    _x0 = _d['L0_attn_hidden_states']
    _d['L0_attn_hidden_states'] = jax.random.normal(jax.random.fold_in(jax.random.key(seed), 1), (16, 256, 128), dtype=_x0.dtype)
    del _x0
    return _d

def reference(L0_attn_hidden_states, L0_attn_rel_pos, L0_attn_Wq, L0_attn_Wk, L0_attn_Wv, L0_attn_Wo, L0_ffn_router_w, L0_ffn_router_b, L0_ffn_W1, L0_ffn_b1, L0_ffn_W2, L0_ffn_b2):

    def _L0_attn_ref(hidden_states, rel_pos, Wq, Wk, Wv, Wo):
        import jax, jax.numpy as jnp
        import numpy as np
        NUM_HEADS = 8
        CHUNK = 64

        def _retention(q, k, v):
            B, Hn, L, DK = q.shape
            DV = v.shape[-1]
            C = CHUNK
            N = L // C
            dt = q.dtype
            gamma = (1.0 - jnp.exp2(-5.0 - jnp.arange(Hn, dtype=jnp.float32))).astype(dt)
            q = q * DK ** (-0.5)
            idx = jnp.arange(C)
            diff = idx[:, None] - idx[None, :]
            D = jnp.where(diff >= 0, gamma[:, None, None] ** diff, 0.0).astype(dt)
            decay_q = (gamma[:, None] ** (idx[None, :] + 1)).astype(dt)
            decay_k = (gamma[:, None] ** (C - 1 - idx[None, :])).astype(dt)
            decay_s = (gamma ** C).astype(dt)

            def to_chunks(x):
                return jnp.moveaxis(x.reshape(B, Hn, N, C, -1), 2, 0)
            qs, ks, vs = map(to_chunks, (q, k, v))

            def step(S, x):
                qc, kc, vc = x
                attn = jnp.einsum('bhid,bhjd->bhij', qc, kc) * D
                o_intra = jnp.einsum('bhij,bhje->bhie', attn, vc)
                o_inter = jnp.einsum('bhid,bhde->bhie', qc * decay_q[None, :, :, None], S)
                S_new = decay_s[None, :, None, None] * S + jnp.einsum('bhjd,bhje->bhde', kc * decay_k[None, :, :, None], vc)
                return (S_new, o_intra + o_inter)
            S0 = jnp.zeros((B, Hn, DK, DV), dt)
            _, o = jax.lax.scan(step, S0, (qs, ks, vs))
            return jnp.moveaxis(o, 0, 2).reshape(B, Hn, L, DV)

        def _xavier(key, fan_in, fan_out, gain=2 ** (-2.5)):
            limit = gain * np.sqrt(6.0 / (fan_in + fan_out))
            return jax.random.uniform(key, (fan_in, fan_out), jnp.float32, -limit, limit)
        B, L, Dm = hidden_states.shape
        Hd = Dm // NUM_HEADS
        q = (hidden_states @ Wq).reshape(B, L, NUM_HEADS, Hd).transpose(0, 2, 1, 3)
        k = (hidden_states @ Wk).reshape(B, L, NUM_HEADS, Hd).transpose(0, 2, 1, 3)
        v = (hidden_states @ Wv).reshape(B, L, NUM_HEADS, Hd).transpose(0, 2, 1, 3)
        o = _retention(q, k, v)
        o = o.transpose(0, 2, 1, 3).reshape(B, L, Dm)
        return o @ Wo

    def _L0_ffn_ref(x, router_w, router_b, W1, b1, W2, b2):
        import jax, jax.numpy as jnp
        import numpy as np
        D_MODEL = 128
        D_FF = 512
        NUM_EXPERTS = 8
        TOP_K = 2
        BATCH = 4
        SEQ = 256
        logits = jnp.einsum('bsd,de->bse', x, router_w) + router_b
        topk_scores, topk_idx = jax.lax.top_k(logits, TOP_K)
        topk_gates = jax.nn.softmax(topk_scores, axis=-1)
        onehot = jax.nn.one_hot(topk_idx, NUM_EXPERTS, dtype=x.dtype)
        combine = jnp.einsum('bsk,bske->bse', topk_gates, onehot)
        combine_e = jnp.moveaxis(combine, -1, 0)

        def expert_step(acc, params):
            w1, bb1, w2, bb2, c = params
            h = jax.nn.relu(jnp.einsum('bsd,df->bsf', x, w1) + bb1)
            y = jnp.einsum('bsf,fd->bsd', h, w2) + bb2
            return (acc + y * c[..., None], None)
        out, _ = jax.lax.scan(expert_step, jnp.zeros_like(x), (W1, b1, W2, b2, combine_e))
        return out
    x = L0_attn_hidden_states
    x = x + 0.5 * _L0_ffn_ref(_layernorm(x, axis=-1), L0_ffn_router_w, L0_ffn_router_b, L0_ffn_W1, L0_ffn_b1, L0_ffn_W2, L0_ffn_b2)
    x = x + _L0_attn_ref(_layernorm(x, axis=-1), L0_attn_rel_pos, L0_attn_Wq, L0_attn_Wk, L0_attn_Wv, L0_attn_Wo)
    x = x + 0.5 * _L0_ffn_ref(_layernorm(x, axis=-1), L0_ffn_router_w, L0_ffn_router_b, L0_ffn_W1, L0_ffn_b1, L0_ffn_W2, L0_ffn_b2)
    return x

_drawn_inputs = setup_inputs


def setup_inputs(seed=0):
    import zlib

    import numpy as np

    out = dict(_drawn_inputs(seed))
    spreads = {'L0_ffn_router_b': (0.0, 0.1), 'L0_ffn_b1': (0.0, 0.365), 'L0_ffn_b2': (0.0, 0.1)}
    factors = {'L0_attn_Wq': 4.192, 'L0_attn_Wk': 4.083, 'L0_attn_Wv': 4.175, 'L0_attn_Wo': 4.113}
    for name, (base, spread) in spreads.items():
        noise = np.random.default_rng([zlib.crc32(name.encode()), seed]).standard_normal(out[name].shape)
        drawn = base * np.exp(spread * noise) if base else spread * noise
        out[name] = jnp.asarray(drawn.astype(out[name].dtype))
    for name, factor in factors.items():
        out[name] = (out[name] * factor).astype(out[name].dtype)
    return out
```

```python
from contextlib import ExitStack

import concourse.bass as bass
from concourse import mybir

FP32 = mybir.dt.float32
FP32R = mybir.dt.float32r
BF16 = mybir.dt.bfloat16
I32 = mybir.dt.int32
U32 = mybir.dt.uint32
ALU = mybir.AluOpType
ACT = mybir.ActivationFunctionType
AXX = mybir.AxisListType.X

SEQS, SEQ_LEN, D = 16, 256, 128
EXPERTS, FF = 8, 512
HEADS = 8
HEAD_DIM = D // HEADS
EPS = 1e-5
TILE = 128
ROWS = SEQS * SEQ_LEN
ROW_TILES = ROWS // TILE
PAIR = SEQ_LEN // TILE
PAIRS = ROW_TILES // PAIR
TOP_K = 2
PICKS = TOP_K * ROW_TILES
FF_CHUNKS = FF // TILE
SLOT_TILES = PICKS + EXPERTS
FAR_BELOW = -3.0e38

CONST_COLUMNS = {}
_at = 0
for _name, _width in (("identity", TILE), ("same_head", D), ("query_decay", TILE), ("key_decay", D),
                      ("before", TILE), ("column", TILE), ("tile_base", PICKS),
                      ("head_rows", HEADS), ("low_first", EXPERTS), ("partition", 1)):
    CONST_COLUMNS[_name] = (_at, _at + _width)
    _at += _width
CONST_WIDTH = _at


class Step:

    def __init__(self, c, turn=None, unroll=1):
        self.c, self.turn, self.unroll = c, turn, unroll

    @property
    def n(self):
        return self.c if self.turn is None else self.turn * self.unroll + self.c

    def after(self, k):
        return Step(self.c + k, self.turn, self.unroll)

    def within(self, count):
        return self.turn is not None or 0 <= self.c < count

    def slot(self, ring):
        return self.c % ring

    def round(self, ring):
        return self.c // ring if self.turn is None else self.turn * (self.unroll // ring) + self.c // ring


def wait_step(eng, sem, step, per=1):
    if step.turn is None and step.c < 0:
        return
    eng.wait_ge(sem, (step.n + 1) * per)


def wait_slot(eng, sems, step, per=16):
    if step.turn is None and step.c < 0:
        return
    ring = len(sems)
    eng.wait_ge(sems[step.slot(ring)], (step.round(ring) + 1) * per)


def run_steps(eng, count, unroll, lag, lead, body, group=None, tail=0):
    first = unroll + lag
    turns = max(0, (count - lead - tail - first) // unroll)
    for c in range(-lead, first):
        body(Step(c))
    if turns:
        with eng.Fori(0, turns) as turn:
            if group is not None:
                group(Step(first, turn, unroll))
            for c in range(first, first + unroll):
                body(Step(c, turn, unroll))
    for c in range(first + turns * unroll, count + lag):
        body(Step(c))


def build(nc, x_in, router_w, router_b, W1, b1, W2, b2, Wq, Wk, Wv, Wo, consts_in, score_decay_in, out):
    ctx = ExitStack()
    with ctx:
        def sb(name, shape, dt=FP32):
            return ctx.enter_context(nc.sbuf_tensor(name, shape, dt))

        def psum(name, width):
            return ctx.enter_context(nc.psum_tensor(name, [TILE, width], FP32))

        def sem(name):
            return ctx.enter_context(nc.semaphore(name))

        def sems(names, suffix):
            return {n: sem(f"{n}_{suffix}") for n in names.split()}

        def ring(name, count):
            return [sem(f"{name}_{i}") for i in range(count)]

        norm_rows = nc.dram_tensor("norm_rows", (ROWS, D), FP32, kind="Internal").ap()
        slot_rows = nc.dram_tensor("slot_rows", (SLOT_TILES * TILE, D), FP32, kind="Internal").ap()

        x = sb("x_rows", [TILE, ROW_TILES * D])
        consts = sb("consts", [TILE, CONST_WIDTH])
        const = {n: consts[:, a:b] for n, (a, b) in CONST_COLUMNS.items()}
        score_decay = sb("score_decay", [TILE, HEADS * TILE])
        w_q = sb("w_q", [D, D])
        w_kv = sb("w_kv", [D, 2 * D])
        w_o = sb("w_o", [D, D])
        w_router = sb("w_router", [D, TILE])
        bias_router = sb("bias_router", [TILE, EXPERTS])
        w1_high = sb("w1_high", [D, EXPERTS * FF], FP32R)
        w1_low = sb("w1_low", [D, EXPERTS * FF], FP32R)
        w1_raw = sb("w1_raw", [D, EXPERTS * FF])
        w2 = sb("w2", [TILE, EXPERTS * FF_CHUNKS * D])
        bias1 = sb("bias1", [TILE, EXPERTS * FF])
        bias2 = sb("bias2", [TILE, EXPERTS * FF])
        before_bf = sb("before_bf", [TILE, TILE], BF16)
        ones_bf = sb("ones_bf", [TILE, TILE], BF16)
        ones_row = sb("ones_row", [TILE, EXPERTS * ROW_TILES])
        column_bf = sb("column_bf", [TILE, TILE], BF16)
        tile_base_bf = sb("tile_base_bf", [TILE, PICKS], BF16)

        wait_carrier = sb("wait_carrier", [TILE, 1])
        stats = sb("stats", [TILE, 2, 2, PAIR, 6])
        moments = sb("moments", [TILE, 2, 2, PAIR, 2])
        var_eps = sb("var_eps", [TILE, 2, 2, PAIR])
        deviation = sb("deviation", [TILE, 2, 2, PAIR])
        inv_dev = sb("inv_dev", [TILE, 2, 2, PAIR])
        norm = sb("norm", [TILE, 2, 2, PAIR * D])
        norm_t = sb("norm_t", [D, 2, 2, PAIR * TILE])
        logits = sb("logits", [TILE, ROW_TILES, EXPERTS])

        def per_expert(name, dt=FP32):
            return sb(name, [TILE, ROW_TILES, EXPERTS], dt)
        best = sb("best", [TILE, TOP_K, ROW_TILES])
        is_best = per_expert("is_best")
        ranked = per_expert("ranked")
        first_rank = sb("first_rank", [TILE, ROW_TILES])
        pick = [per_expert("pick_0"), per_expert("pick_1")]
        other_logits = per_expert("other_logits")
        picked_bf = per_expert("picked_bf", BF16)
        counts = sb("counts", [TILE, EXPERTS, ROW_TILES])
        running = sb("running", [TILE, EXPERTS * ROW_TILES])
        total = sb("total", [TILE, EXPERTS + 1])
        padded_f = sb("padded_f", [TILE, EXPERTS])
        padded_i = sb("padded_i", [TILE, EXPERTS], I32)
        ends = sb("ends", [TILE, EXPERTS + 1])
        shift = sb("shift", [TILE, EXPERTS])
        place = per_expert("place")
        place_f = sb("place_f", [TILE, TOP_K, ROW_TILES])
        place_i = sb("place_i", [TILE, PICKS], I32)
        place_part_i = sb("place_part_i", [TILE, 2, PICKS], I32)
        place_part_bf = sb("place_part_bf", [TILE, 2, PICKS], BF16)
        gap = sb("gap", [TILE, ROW_TILES])
        gap_exp = sb("gap_exp", [TILE, ROW_TILES])
        gap_sum = sb("gap_sum", [TILE, ROW_TILES])
        gate = sb("gate", [TILE, TOP_K, ROW_TILES])
        low_hot = sb("low_hot", [TILE, 2, 4, TILE], BF16)
        high_hot = sb("high_hot", [TILE, 2, 4, SLOT_TILES], BF16)
        high_value = sb("high_value", [TILE, 2, 4, 2 * SLOT_TILES], BF16)
        slot_row_f = sb("slot_row_f", [TILE, SLOT_TILES])
        slot_row = sb("slot_row", [TILE, SLOT_TILES], U32)
        past_end = sb("past_end", [TILE, SLOT_TILES, EXPERTS - 1])
        tile_start = sb("tile_start", [TILE, SLOT_TILES])
        tile_expert_f = sb("tile_expert_f", [TILE, SLOT_TILES])
        expert_offset = sb("expert_offset", [TILE, SLOT_TILES], I32)

        row_index = sb("row_index", [TILE, 4], U32)
        got = sb("got", [TILE, 4, D])
        got_high = sb("got_high", [D, 2, TILE], FP32R)
        got_low = sb("got_low", [D, 2, TILE], FP32R)
        hidden = sb("hidden", [TILE, 2, FF])
        hidden_t = sb("hidden_t", [TILE, 2, FF])
        result = sb("result", [TILE, 4, D])

        back_index = sb("back_index", [TILE, 2 * PAIR * TOP_K], U32)
        back = sb("back", [TILE, 2, TOP_K, PAIR, D])

        q_blocks = w1_raw[:, :].rearrange("p (u h i) -> p u h i", u=2, h=HEADS)
        k_t = sb("k_t", [D, 2, SEQ_LEN])
        q_later = sb("q_later", [D, 2, TILE])
        k_first = sb("k_first", [TILE, 2, D])
        V_STEP = TILE + HEAD_DIM
        v_blocks = sb("v_blocks", [TILE, 2, PAIR, HEADS * V_STEP])
        state = sb("state", [D, 2, D])
        weights = sb("weights", [TILE, PAIR, HEADS * TILE])
        o_t = sb("o_t", [D, SEQ_LEN])

        def v_diagonal(u, c):
            return v_blocks[:, u, c, :].rearrange("p (h s) -> p h s", s=V_STEP)[:, :, 0:HEAD_DIM]

        bank01, bank23 = psum("bank01", 1024), psum("bank23", 1024)
        bank4, bank5, bank6, bank7 = (psum(f"bank{i}", 512) for i in range(4, 8))
        ps_scores = [bank01, bank23]
        ps_got_t = [bank01[:, 0:TILE], bank01[:, 512:512 + TILE]]
        ps_hidden = [bank23[:, 0:512], bank23[:, 512:1024]]
        ps_hidden_t = [bank4, bank5]
        ps_result = [bank6[:, 0:D], bank7[:, 0:D]]

        consts_loaded, weights_loaded, x_loaded = sem("consts_loaded"), sem("weights_loaded"), sem("x_loaded")
        consts_ready, w1_split, zeroed = sem("consts_ready"), sem("w1_split"), sem("zeroed")
        w1_loaded = sem("w1_loaded")
        prep = [sems("stats_done moments_done var_ready dev_ready inv_ready norm_ready norm_t_ps norm_t_ready "
                     "logits_ps logits_ready", f"prep{f}") for f in range(2)]
        rows_stored = [ring(f"rows_stored_prep{f}", 2) for f in range(2)]
        route = [sems("chain picked ranks_ps gap_ready exp_ready hot_low hot_high hot_ready table_ps "
                      "places_ready table_ready", f"route{f}") for f in range(2)]
        expert = [sems("index_copied got_t_ps high_ready low_ready hidden_ps hidden_ready hidden_t_ps "
                       "hidden_t_ready result_ps result_ready", f"ffn{f}") for f in range(2)]
        gathered = [ring(f"gathered_ffn{f}", 4) for f in range(2)]
        result_stored = [ring(f"result_stored_ffn{f}", 4) for f in range(2)]
        back_gathered = [ring(f"back_gathered{f}", 2) for f in range(2)]
        comb = [sems("index_copied first_added added", f"back{f}") for f in range(2)]
        att = sems("stats_done moments_done var_ready dev_ready inv_ready norm_ready norm_t_ps norm_t_ready "
                   "qkv_ps q_ready k_ready kv_ready state_ps state_ready scores_ps0 scores_ps1 weights_ready0 "
                   "weights_ready1 o_ps o_ready proj_ps x_ready", "att")
        out_stored = ring("out_stored", 2)

        SCORES_PS = [att["scores_ps0"], att["scores_ps1"]]
        WEIGHTS_READY = [att["weights_ready0"], att["weights_ready1"]]

        def x_pair(step):
            return x[:, bass.ds(step.n * (PAIR * D), PAIR * D)]

        block = ctx.enter_context(nc.Block())

        @block.sync
        def _(sp):
            sp.dma_start(consts[:, :], consts_in).then_inc(consts_loaded, 16)
            sp.dma_start(x[:, :].rearrange("p (t d) -> p t d", d=D),
                         x_in.rearrange("b (t p) d -> p (b t) d", p=TILE)).then_inc(x_loaded, 16)
            sp.dma_start(w2[:, :].rearrange("p (e c d) -> p e c d", e=EXPERTS, c=FF_CHUNKS),
                         W2.rearrange("e (c p) d -> p e c d", p=TILE)).then_inc(weights_loaded, 16)
            sp.dma_start(bias1[:, :], b1.rearrange("e f -> (e f)").partition_broadcast(TILE))\
              .then_inc(weights_loaded, 16)
            sp.dma_start(bias2[:, :].rearrange("p (e f) -> p e f", e=EXPERTS)[:, :, 0:D],
                         b2.rearrange("e d -> (e d)").partition_broadcast(TILE)
                           .rearrange("p (e d) -> p e d", e=EXPERTS)).then_inc(weights_loaded, 16)

            def store_norm(f, b, which):
                wait_step(sp, prep[f]["norm_ready"], b)
                sp.dma_start(norm_rows[bass.ds(b.n * (PAIR * TILE), PAIR * TILE), :]
                             .rearrange("(t p) d -> p t d", p=TILE),
                             norm[:, which, b.slot(2), :].rearrange("p (t d) -> p t d", d=D))\
                  .then_inc(rows_stored[f][b.slot(2)], 16)

            def store_result(f, j):
                wait_step(sp, expert[f]["result_ready"], j)
                sp.dma_start(slot_rows[bass.ds(j.n * TILE, TILE), :], result[:, j.slot(4), :])\
                  .then_inc(result_stored[f][j.slot(4)], 16)

            def store_out(b):
                wait_step(sp, comb[1]["added"], b, PAIR)
                sp.dma_start(out[bass.ds(b.n, 1), :, :].rearrange("b (t p) d -> p (b t) d", p=TILE),
                             x_pair(b).rearrange("p (t d) -> p t d", d=D)).then_inc(out_stored[b.slot(2)], 16)

            for f in range(2):
                run_steps(sp, PAIRS, 2, 0, 0, lambda b: store_norm(f, b, 1))
                run_steps(sp, SLOT_TILES, 4, 0, 0, lambda j: store_result(f, j))
            run_steps(sp, PAIRS, 2, 0, 0, store_out)
            for s in range(2):
                sp.wait_ge(out_stored[s], PAIRS // 2 * 16)

        @block.gpsimd
        def _(pool):
            nc.gpsimd.memset(v_blocks[:, :, :, :].rearrange("p a b c -> p (a b c)"), 0.0).then_inc(zeroed, 1)

            def copy_row_index(f, j):
                nc.gpsimd.tensor_copy(row_index[:, j.slot(4):j.slot(4) + 1], slot_row[:, bass.ds(j.n, 1)])\
                  .then_inc(expert[f]["index_copied"], 1)

            def gather_tile(f, j):
                wait_step(pool, expert[f]["index_copied"], j)
                wait_step(pool, expert[f]["got_t_ps"], j.after(-4))
                if j.after(1).within(SLOT_TILES):
                    wait_slot(pool, gathered[f], j.after(1 - 4))
                    copy_row_index(f, j.after(1))
                nc.gpsimd.indirect_dma_start(
                    out=got[:, j.slot(4), :], out_offset=None, in_=norm_rows,
                    in_offset=bass.IndirectOffsetOnAxis(ap=row_index[:, j.slot(4):j.slot(4) + 1], axis=0))\
                  .then_inc(gathered[f][j.slot(4)], 16)

            def copy_back_index(f, b):
                u = b.slot(2)
                nc.gpsimd.tensor_copy(
                    back_index[:, u * 4:u * 4 + 4].rearrange("p (k t) -> p k t", k=TOP_K),
                    place_i[:, :].bitcast(U32).rearrange("p (k t) -> p k t", k=TOP_K)
                    [:, :, bass.ds(b.n * PAIR, PAIR)]).then_inc(comb[f]["index_copied"], 1)

            def gather_back(f, b):
                u = b.slot(2)
                wait_step(pool, comb[f]["index_copied"], b)
                wait_step(pool, comb[f]["added"], b.after(-2), PAIR)
                if b.after(1).within(PAIRS):
                    wait_slot(pool, back_gathered[f], b.after(1 - 2), 16 * 4)
                    copy_back_index(f, b.after(1))
                for k in range(TOP_K):
                    for t in range(PAIR):
                        n = u * 4 + k * PAIR + t
                        nc.gpsimd.indirect_dma_start(
                            out=back[:, u, k, t, :], out_offset=None, in_=slot_rows,
                            in_offset=bass.IndirectOffsetOnAxis(ap=back_index[:, n:n + 1], axis=0))\
                          .then_inc(back_gathered[f][u], 16)

            for f in range(2):
                pool.wait_ge(route[f]["table_ready"], 1)
                for s in range(2):
                    pool.wait_ge(rows_stored[f][s], PAIRS // 2 * 16)
                copy_row_index(f, Step(0))
                run_steps(pool, SLOT_TILES, 4, 0, 1, lambda j: gather_tile(f, j) if j.within(SLOT_TILES) else None)
                for s in range(4):
                    pool.wait_ge(result_stored[f][s], SLOT_TILES // 4 * 16)
                copy_back_index(f, Step(0))
                run_steps(pool, PAIRS, 2, 0, 1, lambda b: gather_back(f, b) if b.within(PAIRS) else None)

        @block.scalar
        def _(act):
            act.dma_start(w_q[:, :], Wq).then_inc(weights_loaded, 16)
            act.dma_start(w_kv[:, 0:D], Wk).then_inc(weights_loaded, 16)
            act.dma_start(w_kv[:, D:2 * D], Wv).then_inc(weights_loaded, 16)
            act.dma_start(w_o[:, :], Wo).then_inc(weights_loaded, 16)
            act.dma_start(score_decay[:, :], score_decay_in).then_inc(weights_loaded, 16)
            act.wait_ge(zeroed, 2)
            act.dma_start(w_router[:, 0:EXPERTS], router_w).then_inc(consts_loaded, 16)
            act.dma_start(bias_router[:, :], router_b.partition_broadcast(TILE)).then_inc(consts_loaded, 16)
            act.dma_start(w1_raw[:, :].rearrange("p (e f) -> p e f", e=EXPERTS),
                          W1.rearrange("e p f -> p e f")).then_inc(w1_loaded, 16)

            def sqrt_pair(s, b, which):
                wait_step(act, s["var_ready"], b)
                nc.scalar.activation(deviation[:, which, b.slot(2), :], var_eps[:, which, b.slot(2), :],
                                     ACT.Sqrt).then_inc(s["dev_ready"], 1)

            def copy_norm_t(s, b, which, ps, readers):
                wait_step(act, s["norm_t_ps"], b)
                wait_step(act, readers, b.after(-2))
                nc.scalar.activation(norm_t[:, which, b.slot(2), :], ps, ACT.Copy)\
                  .then_inc(s["norm_t_ready"], 1)

            def first_prep(b):
                if b.after(2).within(PAIRS):
                    sqrt_pair(prep[0], b.after(2), 1)
                if b.within(PAIRS):
                    copy_norm_t(prep[0], b, 1, (bank6, bank7)[b.slot(2)][:, 0:SEQ_LEN], prep[0]["logits_ps"])

            def exp_gap(f):
                act.wait_ge(route[f]["gap_ready"], 1)
                nc.scalar.activation(gap_exp[:, :], gap[:, :], ACT.Exp).then_inc(route[f]["exp_ready"], 1)

            def split_high(f, j):
                wait_step(act, expert[f]["got_t_ps"], j)
                wait_step(act, expert[f]["hidden_ps"], j.after(-2))
                nc.scalar.activation(got_high[:, j.slot(2), :], ps_got_t[j.slot(2)], ACT.Copy)\
                  .then_inc(expert[f]["high_ready"], 1)

            def relu_tile(f, j):
                wait_step(act, expert[f]["hidden_t_ps"], j)
                wait_step(act, expert[f]["result_ps"], j.after(-2))
                nc.scalar.activation(hidden_t[:, j.slot(2), :], ps_hidden_t[j.slot(2)][:, :], ACT.Relu)\
                  .then_inc(expert[f]["hidden_t_ready"], 1)

            def expert_step(f, s):
                if s.after(1).within(SLOT_TILES):
                    relu_tile(f, s.after(1))
                if s.after(4).within(SLOT_TILES):
                    split_high(f, s.after(4))

            def copy_queries(b):
                u = b.slot(2)
                wait_step(act, att["qkv_ps"], b)
                wait_step(act, SCORES_PS[1], b.after(-2))
                for h in range(HEADS):
                    last = nc.scalar.activation(q_blocks[:, u, h, :], bank4[:, 0:SEQ_LEN], ACT.Copy,
                                                scale=const["head_rows"][:, h:h + 1])
                last.then_inc(att["q_ready"], 1)
                nc.scalar.activation(k_t[:, u, :], bank4[:, SEQ_LEN:2 * SEQ_LEN], ACT.Copy)\
                  .then_inc(att["k_ready"], 1)

            def copy_o(b):
                wait_step(act, att["o_ps"], b)
                wait_step(act, att["proj_ps"], b.after(-1))
                nc.scalar.activation(o_t[:, :], bank7[:, 0:SEQ_LEN], ACT.Copy).then_inc(att["o_ready"], 1)

            def middle(s):
                if s.after(1).within(PAIRS):
                    copy_norm_t(att, s.after(1), 0, bank6[:, 0:SEQ_LEN], att["qkv_ps"])
                    copy_queries(s.after(1))
                if s.after(2).within(PAIRS):
                    sqrt_pair(att, s.after(2), 0)
                if s.within(PAIRS):
                    copy_o(s)
                    sqrt_pair(prep[1], s, 1)
                if s.after(-1).within(PAIRS):
                    copy_norm_t(prep[1], s.after(-1), 1, bank6[:, SEQ_LEN:2 * SEQ_LEN], prep[1]["logits_ps"])

            act.wait_ge(consts_loaded, 48)
            run_steps(act, PAIRS, 2, 0, 2, first_prep)
            act.wait_ge(w1_loaded, 16)
            nc.scalar.activation(w1_high[:, :], w1_raw[:, :], ACT.Copy).then_inc(w1_split, 1)
            exp_gap(0)
            run_steps(act, SLOT_TILES, 4, 0, 4, lambda s: expert_step(0, s))
            run_steps(act, PAIRS, 2, 1, 2, middle)
            exp_gap(1)
            run_steps(act, SLOT_TILES, 4, 0, 4, lambda s: expert_step(1, s))

        @block.vector
        def _(dve):
            nc.vector.memset(w_router[:, :], 0.0).then_inc(zeroed, 1)
            nc.vector.memset(ones_bf[:, :], 1.0)
            nc.vector.memset(ones_row[:, :], 1.0)
            nc.vector.memset(total[:, 0:1], 0.0)
            nc.vector.memset(ends[:, 0:1], 0.0)
            dve.wait_ge(consts_loaded, 48)
            nc.vector.tensor_copy(before_bf[:, :], const["before"])
            nc.vector.tensor_copy(column_bf[:, :], const["column"])
            nc.vector.tensor_copy(tile_base_bf[:, :], const["tile_base"])
            nc.vector.tensor_scalar(tile_start[:, :], const["column"][:, 0:SLOT_TILES], float(TILE), None, ALU.mult)\
              .then_inc(consts_ready, 1)

            def carry_wait():
                nc.vector.memset(wait_carrier[:, :], 0.0)

            def take_stats(s, b, which):
                u = b.slot(2)
                carry_wait()
                for t in range(PAIR):
                    last = nc.vector.bn_stats(stats[:, which, u, t, :], x[:, bass.ds((b.n * PAIR + t) * D, D)])
                last.then_inc(s["stats_done"], 1)
                wait_step(dve, s["stats_done"], b)
                carry_wait()
                for t in range(PAIR):
                    last = nc.vector.bn_aggr(moments[:, which, u, t, :], stats[:, which, u, t, :])
                last.then_inc(s["moments_done"], 1)
                wait_step(dve, s["moments_done"], b)
                nc.vector.tensor_scalar(var_eps[:, which, u, :], moments[:, which, u, :, 1], EPS, None, ALU.add)\
                  .then_inc(s["var_ready"], 1)

            def normalise(s, b, which, reader, stored=None):
                u = b.slot(2)
                wait_step(dve, s["dev_ready"], b)
                nc.vector.reciprocal(inv_dev[:, which, u, :], deviation[:, which, u, :]).then_inc(s["inv_ready"], 1)
                wait_step(dve, s["inv_ready"], b)
                wait_step(dve, reader, b.after(-2))
                if stored is not None:
                    wait_slot(dve, stored, b.after(-2))
                for t in range(PAIR):
                    last = nc.vector.tensor_scalar(norm[:, which, u, t * D:(t + 1) * D],
                                                   x[:, bass.ds((b.n * PAIR + t) * D, D)],
                                                   moments[:, which, u, t, 0:1], inv_dev[:, which, u, t:t + 1],
                                                   ALU.subtract, ALU.mult)
                last.then_inc(s["norm_ready"], 1)

            def add_router_bias(s, b, ps):
                wait_step(dve, s["logits_ps"], b)
                nc.vector.tensor_tensor(
                    logits[:, bass.ds(b.n * PAIR, PAIR), :],
                    ps.rearrange("p (t c) -> p t c", t=PAIR)[:, :, 0:EXPERTS],
                    bias_router[:, :].unsqueeze(1).to_broadcast([TILE, PAIR, EXPERTS]), ALU.add)\
                  .then_inc(s["logits_ready"], 1)

            def first_prep(b):
                if b.after(2).within(PAIRS):
                    take_stats(prep[0], b.after(2), 1)
                if b.after(1).within(PAIRS):
                    normalise(prep[0], b.after(1), 1, prep[0]["norm_t_ps"], rows_stored[0])
                if b.after(-1).within(PAIRS):
                    add_router_bias(prep[0], b.after(-1),
                                    (bank6, bank7)[b.after(-1).slot(2)][:, SEQ_LEN:2 * SEQ_LEN])

            def route_rows(f):
                r = route[f]
                done = [0]

                def link(ins):
                    done[0] += 1
                    ins.then_inc(r["chain"], 1)
                    dve.wait_ge(r["chain"], done[0])

                def over_experts(a):
                    return a.unsqueeze(2).to_broadcast([TILE, ROW_TILES, EXPERTS])

                rank = const["low_first"].unsqueeze(1).to_broadcast([TILE, ROW_TILES, EXPERTS])
                scores = logits
                for k in range(TOP_K):
                    link(nc.vector.tensor_reduce(best[:, k, :], scores[:, :, :], AXX, ALU.max))
                    link(nc.vector.tensor_tensor(is_best[:, :, :], scores[:, :, :], over_experts(best[:, k, :]),
                                                 ALU.is_equal))
                    link(nc.vector.tensor_tensor(ranked[:, :, :], is_best[:, :, :], rank, ALU.mult))
                    link(nc.vector.tensor_reduce(first_rank[:, :], ranked[:, :, :], AXX, ALU.max))
                    link(nc.vector.tensor_tensor(pick[k][:, :, :], over_experts(first_rank[:, :]), rank,
                                                 ALU.is_equal))
                    if k == 0:
                        link(nc.vector.scalar_tensor_tensor(other_logits[:, :, :], pick[0][:, :, :], FAR_BELOW,
                                                            logits[:, :, :], ALU.mult, ALU.add))
                        scores = other_logits
                nc.vector.tensor_tensor(picked_bf[:, :, :], pick[0][:, :, :], pick[1][:, :, :], ALU.add)\
                  .then_inc(r["picked"], 1)
                nc.vector.tensor_tensor(gap[:, :], best[:, 1, :], best[:, 0, :], ALU.subtract)\
                  .then_inc(r["gap_ready"], 1)
                dve.wait_ge(r["ranks_ps"], 1)
                link(nc.vector.tensor_copy(counts[:, :, :],
                                           bank4[:, 256:512].rearrange("p (t e) -> p e t", e=EXPERTS)))
                link(nc.vector.tensor_tensor_scan(running[:, :], ones_row[:, :],
                                                  counts[:, :, :].rearrange("p e t -> p (e t)"), 0.0,
                                                  ALU.mult, ALU.add))
                running_e = running[:, :].rearrange("p (e t) -> p e t", e=EXPERTS)
                nc.vector.tensor_copy(total[:, 1:EXPERTS + 1], running_e[:, :, ROW_TILES - 1])
                link(nc.vector.tensor_tensor(counts[:, :, :], running_e, counts[:, :, :], ALU.subtract))
                link(nc.vector.scalar_tensor_tensor(padded_i[:, :], total[:, 1:EXPERTS + 1], float(TILE - 1),
                                                    total[:, 0:EXPERTS], ALU.add, ALU.subtract))
                link(nc.vector.tensor_scalar(padded_i[:, :], padded_i[:, :], -TILE, None, ALU.bitwise_and))
                link(nc.vector.tensor_copy(padded_f[:, :], padded_i[:, :]))
                link(nc.vector.tensor_tensor_scan(ends[:, 1:EXPERTS + 1], ones_row[:, 0:EXPERTS], padded_f[:, :],
                                                  0.0, ALU.mult, ALU.add))
                link(nc.vector.tensor_tensor(shift[:, :], ends[:, 0:EXPERTS], total[:, 0:EXPERTS], ALU.subtract))
                link(nc.vector.tensor_tensor(counts[:, :, :], counts[:, :, :],
                                             shift[:, :].unsqueeze(2).to_broadcast([TILE, EXPERTS, ROW_TILES]),
                                             ALU.add))
                link(nc.vector.tensor_tensor(place[:, :, :],
                                             bank4[:, 0:256].rearrange("p (t e) -> p t e", e=EXPERTS),
                                             counts[:, :, :].rearrange("p e t -> p t e"), ALU.add))
                for k in range(TOP_K):
                    link(nc.vector.tensor_tensor(ranked[:, :, :], pick[k][:, :, :], place[:, :, :], ALU.mult))
                    link(nc.vector.tensor_reduce(place_f[:, k, :], ranked[:, :, :], AXX, ALU.add))
                link(nc.vector.tensor_copy(place_i[:, :], place_f[:, :, :].rearrange("p k t -> p (k t)")))
                nc.vector.tensor_scalar(place_part_i[:, 0, :], place_i[:, :], TILE - 1, None, ALU.bitwise_and)
                link(nc.vector.tensor_scalar(place_part_i[:, 1, :], place_i[:, :], TILE.bit_length() - 1, None,
                                             ALU.logical_shift_right))
                link(nc.vector.tensor_copy(place_part_bf[:, :, :], place_part_i[:, :, :]))

                def hot_group(g):
                    u = g.slot(2)
                    wait_step(dve, r["table_ps"], g.after(-2))
                    nc.vector.tensor_tensor(
                        low_hot[:, u, :, :], column_bf[:, :].unsqueeze(1).to_broadcast([TILE, 4, TILE]),
                        place_part_bf[:, 0, bass.ds(g.n * 4, 4)].unsqueeze(2).to_broadcast([TILE, 4, TILE]),
                        ALU.is_equal)
                    nc.vector.tensor_tensor(
                        high_hot[:, u, :, :],
                        column_bf[:, 0:SLOT_TILES].unsqueeze(1).to_broadcast([TILE, 4, SLOT_TILES]),
                        place_part_bf[:, 1, bass.ds(g.n * 4, 4)].unsqueeze(2).to_broadcast([TILE, 4, SLOT_TILES]),
                        ALU.is_equal).then_inc(r["hot_high"], 1)
                    wait_step(dve, r["hot_high"], g)
                    nc.vector.tensor_tensor(
                        high_value[:, u, :, 0:SLOT_TILES], high_hot[:, u, :, :],
                        tile_base_bf[:, bass.ds(g.n * 4, 4)].unsqueeze(2).to_broadcast([TILE, 4, SLOT_TILES]),
                        ALU.mult)
                    nc.vector.tensor_scalar(high_value[:, u, :, SLOT_TILES:2 * SLOT_TILES], high_hot[:, u, :, :],
                                            const["partition"], None, ALU.mult).then_inc(r["hot_ready"], 1)

                run_steps(dve, PICKS // 4, 2, 0, 0, hot_group)
                dve.wait_ge(r["exp_ready"], 1)
                link(nc.vector.tensor_scalar(gap_sum[:, :], gap_exp[:, :], 2.0, 2.0, ALU.mult, ALU.add))
                link(nc.vector.reciprocal(gate[:, 0, :], gap_sum[:, :]))
                link(nc.vector.tensor_tensor(gate[:, 1, :], gate[:, 0, :], gap_exp[:, :], ALU.mult))
                link(nc.vector.tensor_tensor(
                    past_end[:, :, :], tile_start[:, :].unsqueeze(2).to_broadcast([TILE, SLOT_TILES, EXPERTS - 1]),
                    ends[:, 1:EXPERTS].unsqueeze(1).to_broadcast([TILE, SLOT_TILES, EXPERTS - 1]), ALU.is_ge))
                link(nc.vector.tensor_reduce(tile_expert_f[:, :], past_end[:, :, :], AXX, ALU.add))
                link(nc.vector.tensor_scalar(expert_offset[:, :], tile_expert_f[:, :], float(FF), None, ALU.mult))
                dve.wait_ge(r["table_ps"], PICKS // 4)
                link(nc.vector.tensor_copy(slot_row_f[:, :], bank5[:, 0:SLOT_TILES]))
                nc.vector.tensor_tensor(slot_row[:, :], slot_row_f[:, :], bank5[:, SLOT_TILES:2 * SLOT_TILES],
                                        ALU.add).then_inc(r["table_ready"], 1)

            offsets = {}

            def load_offsets(first, count):
                _, values = nc.values_load_multi_w_load_instructions(
                    expert_offset[0:1, bass.ds(first.n, count)], engines=[mybir.EngineType.DVE], min_val=0,
                    max_val=(EXPERTS - 1) * FF,
                    skip_runtime_bounds_check_because="a sum of EXPERTS - 1 comparisons times FF")
                for i in range(count):
                    offsets[first.turn is None, first.c + i] = values[i]

            def offset(j):
                key = (j.turn is None, j.c)
                if key not in offsets:
                    load_offsets(j, 1)
                return offsets[key]

            def add_bias1(f, j):
                at = offset(j)
                wait_step(dve, expert[f]["hidden_ps"], j)
                wait_step(dve, expert[f]["hidden_t_ps"], j.after(-2))
                nc.vector.tensor_tensor(hidden[:, j.slot(2), :], ps_hidden[j.slot(2)], bias1[:, bass.ds(at, FF)],
                                        ALU.add).then_inc(expert[f]["hidden_ready"], 1)

            def add_bias2(f, j):
                at = offset(j)
                wait_step(dve, expert[f]["result_ps"], j)
                wait_slot(dve, result_stored[f], j.after(-4))
                nc.vector.tensor_tensor(result[:, j.slot(4), :], ps_result[j.slot(2)], bias2[:, bass.ds(at, D)],
                                        ALU.add).then_inc(expert[f]["result_ready"], 1)

            def split_low(f, j):
                wait_step(dve, expert[f]["high_ready"], j)
                wait_step(dve, expert[f]["hidden_ps"], j.after(-2))
                nc.vector.tensor_tensor(got_low[:, j.slot(2), :], ps_got_t[j.slot(2)],
                                        got_high[:, j.slot(2), :].bitcast(FP32), ALU.subtract)\
                  .then_inc(expert[f]["low_ready"], 1)

            def expert_step(f, s):
                if s.after(2).within(SLOT_TILES):
                    add_bias1(f, s.after(2))
                if s.within(SLOT_TILES):
                    add_bias2(f, s)
                if s.after(4).within(SLOT_TILES):
                    split_low(f, s.after(4))

            def run_experts(f):
                offsets.clear()
                run_steps(dve, SLOT_TILES, 4, 0, 4, lambda s: expert_step(f, s),
                          group=lambda first: load_offsets(first, 6))

            def add_back(f, b):
                u = b.slot(2)
                wait_slot(dve, back_gathered[f], b, 16 * 4)
                for k in range(TOP_K):
                    if k:
                        wait_step(dve, comb[f]["first_added"], b, PAIR)
                    for t in range(PAIR):
                        row = x[:, bass.ds((b.n * PAIR + t) * D, D)]
                        nc.vector.scalar_tensor_tensor(row, back[:, u, k, t, :],
                                                       gate[:, k, bass.ds(b.n * PAIR + t, 1)], row,
                                                       ALU.mult, ALU.add)\
                          .then_inc(comb[f]["added" if k else "first_added"], 1)

            def weigh_scores(b):
                for c in range(PAIR):
                    wait_step(dve, SCORES_PS[c], b)
                    wait_step(dve, att["o_ps"], b.after(-1))
                    nc.vector.tensor_tensor(weights[:, c, :], ps_scores[c][:, :], score_decay[:, :], ALU.mult)\
                      .then_inc(WEIGHTS_READY[c], 1)

            def copy_keys_values(b):
                u = b.slot(2)
                wait_step(dve, att["k_ready"], b)
                wait_step(dve, att["o_ps"], b.after(-2))
                nc.vector.tensor_tensor(q_later[:, u, :], bank4[:, TILE:SEQ_LEN], const["query_decay"], ALU.mult)
                nc.vector.tensor_tensor(k_first[:, u, :], bank5[:, 0:D], const["key_decay"], ALU.mult)
                for c in range(PAIR):
                    last = nc.vector.tensor_copy(v_diagonal(u, c), bank5[:, D * (1 + c):D * (2 + c)]
                                                 .rearrange("p (h e) -> p h e", h=HEADS))
                last.then_inc(att["kv_ready"], 1)

            def mask_state(b):
                wait_step(dve, att["state_ps"], b)
                nc.vector.tensor_tensor(state[:, b.slot(2), :], bank5[:, 3 * D:4 * D], const["same_head"], ALU.mult)\
                  .then_inc(att["state_ready"], 1)

            def add_projection(b):
                wait_step(dve, att["proj_ps"], b)
                nc.vector.tensor_tensor(x_pair(b), x_pair(b), bank7[:, SEQ_LEN:2 * SEQ_LEN], ALU.add)\
                  .then_inc(att["x_ready"], 1)

            def middle(s):
                if s.within(PAIRS):
                    weigh_scores(s)
                if s.after(-2).within(PAIRS):
                    add_router_bias(prep[1], s.after(-2), bank6[:, SEQ_LEN:2 * SEQ_LEN])
                if s.after(1).within(PAIRS):
                    copy_keys_values(s.after(1))
                if s.after(1).within(PAIRS):
                    mask_state(s.after(1))
                if s.after(2).within(PAIRS):
                    add_back(0, s.after(2))
                    wait_step(dve, comb[0]["added"], s.after(2), PAIR)
                    take_stats(att, s.after(2), 0)
                if s.within(PAIRS):
                    add_projection(s)
                    wait_step(dve, att["x_ready"], s)
                    take_stats(prep[1], s, 1)
                if s.after(2).within(PAIRS):
                    normalise(att, s.after(2), 0, att["norm_t_ps"])
                if s.within(PAIRS):
                    normalise(prep[1], s, 1, prep[1]["norm_t_ps"], rows_stored[1])

            dve.wait_ge(consts_ready, 1)
            dve.wait_ge(x_loaded, 16)
            run_steps(dve, PAIRS, 2, 1, 2, first_prep)
            dve.wait_ge(prep[0]["logits_ready"], PAIRS)
            dve.wait_ge(w1_split, 1)
            nc.vector.tensor_tensor(w1_low[:, :], w1_raw[:, :], w1_high[:, :].bitcast(FP32), ALU.subtract)\
              .then_inc(w1_split, 1)
            route_rows(0)
            dve.wait_ge(route[0]["table_ready"], 1)
            dve.wait_ge(weights_loaded, 16 * 8)
            dve.wait_ge(zeroed, 2)
            run_experts(0)
            run_steps(dve, PAIRS, 2, 2, 2, middle)
            dve.wait_ge(prep[1]["logits_ready"], PAIRS)
            route_rows(1)
            dve.wait_ge(route[1]["table_ready"], 1)
            run_experts(1)
            run_steps(dve, PAIRS, 2, 0, 0, lambda b: add_back(1, b))

        @block.tensor
        def _(pe):
            identity = const["identity"]

            def transpose_norm(s, b, which, ps):
                wait_step(pe, s["norm_ready"], b)
                for t in range(PAIR):
                    last = nc.tensor.transpose(ps[:, t * TILE:(t + 1) * TILE],
                                               norm[:, which, b.slot(2), t * D:(t + 1) * D], identity)
                last.then_inc(s["norm_t_ps"], 1)

            def router(s, b, ps):
                wait_step(pe, s["norm_t_ready"], b)
                for t in range(PAIR):
                    last = nc.tensor.matmul(ps[:, t * TILE:(t + 1) * TILE],
                                            norm_t[:, 1, b.slot(2), t * TILE:(t + 1) * TILE], w_router[:, :],
                                            start=True, stop=True)
                last.then_inc(s["logits_ps"], 1)

            def first_prep(s):
                b = s.after(1)
                if b.within(PAIRS):
                    wait_step(pe, prep[0]["logits_ready"], b.after(-2))
                    transpose_norm(prep[0], b, 1, (bank6, bank7)[b.slot(2)][:, 0:SEQ_LEN])
                if s.within(PAIRS):
                    router(prep[0], s, (bank6, bank7)[s.slot(2)][:, SEQ_LEN:2 * SEQ_LEN])

            def route_rows(f):
                r = route[f]
                pe.wait_ge(r["picked"], 1)
                flat = picked_bf[:, :, :].rearrange("p t e -> p (t e)")
                nc.tensor.matmul(bank4[:, 0:256], before_bf[:, :], flat, start=True, stop=True)
                nc.tensor.matmul(bank4[:, 256:512], ones_bf[:, :], flat, start=True, stop=True)\
                  .then_inc(r["ranks_ps"], 1)

                def table_group(g):
                    u = g.slot(2)
                    wait_step(pe, r["hot_ready"], g)
                    for i in range(4):
                        last = nc.tensor.matmul(bank5[:, 0:2 * SLOT_TILES], low_hot[:, u, i, :],
                                                high_value[:, u, i, :],
                                                start=g.turn is None and g.c == 0 and i == 0,
                                                stop=g.turn is None and g.c == PICKS // 4 - 1 and i == 3)
                    last.then_inc(r["table_ps"], 1)

                run_steps(pe, PICKS // 4, 2, 0, 0, table_group, tail=2)

            offsets = {}

            def load_offsets(first, count):
                _, values = nc.values_load_multi_w_load_instructions(
                    expert_offset[0:1, bass.ds(first.n, count)], engines=[mybir.EngineType.PE], min_val=0,
                    max_val=(EXPERTS - 1) * FF,
                    skip_runtime_bounds_check_because="a sum of EXPERTS - 1 comparisons times FF")
                for i in range(count):
                    offsets[first.turn is None, first.c + i] = values[i]

            def offset(j):
                key = (j.turn is None, j.c)
                if key not in offsets:
                    load_offsets(j, 1)
                return offsets[key]

            def transpose_got(f, j):
                wait_slot(pe, gathered[f], j)
                wait_step(pe, expert[f]["low_ready"], j.after(-2))
                nc.tensor.transpose(ps_got_t[j.slot(2)], got[:, j.slot(4), :], identity)\
                  .then_inc(expert[f]["got_t_ps"], 1)

            def first_product(f, j):
                at, u = offset(j), j.slot(2)
                wait_step(pe, expert[f]["low_ready"], j)
                wait_step(pe, expert[f]["hidden_ready"], j.after(-2))
                parts = ((got_high, w1_high), (got_high, w1_low), (got_low, w1_high))
                for n, (rows, w) in enumerate(parts):
                    last = nc.tensor.matmul(ps_hidden[u], rows[:, u, :], w[:, bass.ds(at, FF)],
                                            start=n == 0, stop=n == len(parts) - 1)
                last.then_inc(expert[f]["hidden_ps"], 1)

            def transpose_hidden(f, j):
                u = j.slot(2)
                wait_step(pe, expert[f]["hidden_ready"], j)
                wait_step(pe, expert[f]["hidden_t_ready"], j.after(-2))
                for c in range(FF_CHUNKS):
                    last = nc.tensor.transpose(ps_hidden_t[u][:, c * TILE:(c + 1) * TILE],
                                               hidden[:, u, c * TILE:(c + 1) * TILE], identity)
                last.then_inc(expert[f]["hidden_t_ps"], 1)

            def second_product(f, j):
                at, u = offset(j), j.slot(2)
                wait_step(pe, expert[f]["hidden_t_ready"], j)
                wait_step(pe, expert[f]["result_ready"], j.after(-2))
                for c in range(FF_CHUNKS):
                    last = nc.tensor.matmul(ps_result[u], hidden_t[:, u, c * TILE:(c + 1) * TILE],
                                            w2[:, bass.ds(at + c * D, D)], start=c == 0, stop=c == FF_CHUNKS - 1)
                last.then_inc(expert[f]["result_ps"], 1)

            def expert_step(f, s):
                if s.after(2).within(SLOT_TILES):
                    first_product(f, s.after(2))
                if s.after(1).within(SLOT_TILES):
                    transpose_hidden(f, s.after(1))
                if s.within(SLOT_TILES):
                    second_product(f, s)
                if s.after(4).within(SLOT_TILES):
                    transpose_got(f, s.after(4))

            def run_experts(f):
                pe.wait_ge(route[f]["table_ready"], 1)
                offsets.clear()
                run_steps(pe, SLOT_TILES, 4, 0, 4, lambda s: expert_step(f, s),
                          group=lambda first: load_offsets(first, 6))

            def project(b):
                u = b.slot(2)
                wait_step(pe, att["norm_t_ready"], b)
                wait_step(pe, att["state_ready"], b.after(-1))
                xt = norm_t[:, 0, u, :]
                nc.tensor.matmul(bank4[:, 0:SEQ_LEN], w_q[:, :], xt, start=True, stop=True)
                nc.tensor.matmul(bank4[:, SEQ_LEN:2 * SEQ_LEN], w_kv[:, 0:D], xt, start=True, stop=True)
                nc.tensor.matmul(bank5[:, 0:2 * D], xt[:, 0:TILE], w_kv[:, :], start=True, stop=True)
                nc.tensor.matmul(bank5[:, 2 * D:3 * D], xt[:, TILE:SEQ_LEN], w_kv[:, D:2 * D], start=True, stop=True)\
                  .then_inc(att["qkv_ps"], 1)

            def make_state(b):
                u = b.slot(2)
                wait_step(pe, att["kv_ready"], b)
                nc.tensor.matmul(bank5[:, 3 * D:4 * D], k_first[:, u, :], v_diagonal(u, 0), start=True, stop=True)\
                  .then_inc(att["state_ps"], 1)

            def score(b, c):
                u = b.slot(2)
                wait_step(pe, att["k_ready"], b)
                wait_step(pe, WEIGHTS_READY[c], b.after(-1))
                for g in range(2):
                    last = nc.tensor.matmul(ps_scores[c][:, g * 512:(g + 1) * 512],
                                            k_t[:, u, c * TILE:(c + 1) * TILE],
                                            q_blocks[:, u, g * 4:(g + 1) * 4, c * TILE:(c + 1) * TILE],
                                            start=True, stop=True)
                last.then_inc(SCORES_PS[c], 1)

            def mix_values(b):
                u = b.slot(2)
                wait_step(pe, att["x_ready"], b.after(-1))
                for c in range(PAIR):
                    wait_step(pe, WEIGHTS_READY[c], b)
                    if c:
                        wait_step(pe, att["state_ready"], b)
                        nc.tensor.matmul(bank7[:, TILE:SEQ_LEN], state[:, u, :], q_later[:, u, :],
                                         start=True, stop=False)
                    for h in range(HEADS):
                        last = nc.tensor.matmul(bank7[:, c * TILE:(c + 1) * TILE],
                                                v_blocks[:, u, c, h * TILE:(h + 1) * TILE],
                                                weights[:, c, h * TILE:(h + 1) * TILE],
                                                start=c == 0 and h == 0, stop=h == HEADS - 1)
                last.then_inc(att["o_ps"], 1)

            def project_out(b):
                wait_step(pe, att["o_ready"], b)
                for c in range(PAIR):
                    last = nc.tensor.matmul(bank7[:, SEQ_LEN + c * D:SEQ_LEN + (c + 1) * D],
                                            o_t[:, c * TILE:(c + 1) * TILE], w_o[:, :], start=True, stop=True)
                last.then_inc(att["proj_ps"], 1)

            def middle(s):
                if s.within(PAIRS):
                    for c in range(PAIR):
                        score(s, c)
                if s.after(1).within(PAIRS):
                    wait_step(pe, prep[1]["logits_ready"], s.after(-2))
                    transpose_norm(att, s.after(1), 0, bank6[:, 0:SEQ_LEN])
                    project(s.after(1))
                    make_state(s.after(1))
                if s.within(PAIRS):
                    mix_values(s)
                    project_out(s)
                if s.after(-1).within(PAIRS):
                    wait_step(pe, prep[1]["logits_ready"], s.after(-2))
                    transpose_norm(prep[1], s.after(-1), 1, bank6[:, SEQ_LEN:2 * SEQ_LEN])
                    router(prep[1], s.after(-1), bank6[:, SEQ_LEN:2 * SEQ_LEN])

            pe.wait_ge(consts_ready, 1)
            run_steps(pe, PAIRS, 2, 0, 1, first_prep)
            route_rows(0)
            pe.wait_ge(w1_split, 2)
            pe.wait_ge(weights_loaded, 16 * 8)
            run_experts(0)
            pe.wait_ge(zeroed, 2)
            run_steps(pe, PAIRS, 2, 1, 1, middle)
            route_rows(1)
            run_experts(1)


def shape_constants():
    import numpy as np

    i = np.arange(TILE, dtype=np.float64)
    head = np.arange(D) // HEAD_DIM
    gamma = 1.0 - np.exp2(-5.0 - np.arange(HEADS, dtype=np.float64))
    scale = float(HEAD_DIM) ** -0.5
    parts = {
        "identity": np.eye(TILE),
        "same_head": head[:, None] == head[None, :],
        "query_decay": scale * gamma[head][:, None] ** (i[None, :] + 1),
        "key_decay": gamma[head][None, :] ** (TILE - 1 - i[:, None]),
        "before": i[:, None] < i[None, :],
        "column": np.broadcast_to(i[None, :], (TILE, TILE)),
        "tile_base": np.broadcast_to((np.arange(PICKS) % ROW_TILES * TILE)[None, :], (TILE, PICKS)),
        "head_rows": head[:, None] == np.arange(HEADS)[None, :],
        "low_first": np.broadcast_to((EXPERTS - np.arange(EXPERTS))[None, :], (TILE, EXPERTS)),
        "partition": i[:, None],
    }
    table = np.zeros((TILE, CONST_WIDTH), np.float32)
    for name, (a, b) in CONST_COLUMNS.items():
        table[:, a:b] = parts[name]
    distance = i[None, None, :] - i[:, None, None]
    decay = np.where(distance >= 0, scale * gamma[None, :, None] ** np.maximum(distance, 0), 0.0)
    return table, decay.reshape(TILE, HEADS * TILE).astype(np.float32)


def kernel(L0_attn_hidden_states, L0_attn_rel_pos, L0_attn_Wq, L0_attn_Wk, L0_attn_Wv, L0_attn_Wo,
           L0_ffn_router_w, L0_ffn_router_b, L0_ffn_W1, L0_ffn_b1, L0_ffn_W2, L0_ffn_b2):
    import numpy as np
    import concourse.bacc as bacc
    from concourse.bass_utils import run_bass_kernel_spmd

    table, decay = shape_constants()
    arrays = {
        "hidden_states": L0_attn_hidden_states, "router_w": L0_ffn_router_w, "router_b": L0_ffn_router_b,
        "W1": L0_ffn_W1, "b1": L0_ffn_b1, "W2": L0_ffn_W2, "b2": L0_ffn_b2,
        "Wq": L0_attn_Wq, "Wk": L0_attn_Wk, "Wv": L0_attn_Wv, "Wo": L0_attn_Wo,
        "consts": table, "score_decay": decay,
    }
    arrays = {f"in_{n}": np.ascontiguousarray(a) for n, a in arrays.items()}
    nc = bacc.Bacc("TRN2", target_bir_lowering=False, num_devices=1)
    ins = [nc.dram_tensor(n, a.shape, mybir.dt.from_np(a.dtype), kind="ExternalInput").ap()
           for n, a in arrays.items()]
    out = nc.dram_tensor("out_rows", (SEQS, SEQ_LEN, D), FP32, kind="ExternalOutput").ap()
    build(nc, *ins, out)
    return run_bass_kernel_spmd(nc, [arrays], core_ids=[0]).results[0]["out_rows"]
```

```python
from contextlib import ExitStack

import concourse.bass as bass
from concourse import mybir

FP32 = mybir.dt.float32
FP32R = mybir.dt.float32r
BF16 = mybir.dt.bfloat16
I32 = mybir.dt.int32
U32 = mybir.dt.uint32
ALU = mybir.AluOpType
ACT = mybir.ActivationFunctionType
AXX = mybir.AxisListType.X

SEQS, SEQ_LEN, D = 16, 256, 128
EXPERTS, FF = 8, 512
HEADS = 8
HEAD_DIM = D // HEADS
EPS = 1e-5
TILE = 128
ROWS = SEQS * SEQ_LEN
ROW_TILES = ROWS // TILE
PAIR = SEQ_LEN // TILE
PAIRS = ROW_TILES // PAIR
TOP_K = 2
PICKS = TOP_K * ROW_TILES
FF_CHUNKS = FF // TILE
SLOT_TILES = PICKS + EXPERTS
FAR_BELOW = -3.0e38
AHEAD = 7
NOWHERE = float(1 << 20)

CONST_COLUMNS = {}
_at = 0
for _name, _width in (("identity", TILE), ("same_head", D), ("query_decay", TILE), ("key_decay", D),
                      ("before", TILE), ("column", TILE), ("tile_base", PICKS),
                      ("head_rows", HEADS), ("low_first", EXPERTS), ("partition", 1)):
    CONST_COLUMNS[_name] = (_at, _at + _width)
    _at += _width
CONST_WIDTH = _at


class Step:

    def __init__(self, c, turn=None, unroll=1):
        self.c, self.turn, self.unroll = c, turn, unroll

    @property
    def n(self):
        return self.c if self.turn is None else self.turn * self.unroll + self.c

    def after(self, k):
        return Step(self.c + k, self.turn, self.unroll)

    def within(self, count):
        return self.turn is not None or 0 <= self.c < count

    def slot(self, ring):
        return self.c % ring

    def round(self, ring):
        return self.c // ring if self.turn is None else self.turn * (self.unroll // ring) + self.c // ring


def wait_step(eng, sem, step, per=1):
    if step.turn is None and step.c < 0:
        return
    eng.wait_ge(sem, (step.n + 1) * per)


def wait_slot(eng, sems, step, per=16):
    if step.turn is None and step.c < 0:
        return
    ring = len(sems)
    eng.wait_ge(sems[step.slot(ring)], (step.round(ring) + 1) * per)


def run_steps(eng, count, unroll, lag, lead, body, group=None, tail=0):
    first = unroll + lag
    turns = max(0, (count - lead - tail - first) // unroll)
    for c in range(-lead, first):
        body(Step(c))
    if turns:
        with eng.Fori(0, turns) as turn:
            if group is not None:
                group(Step(first, turn, unroll))
            for c in range(first, first + unroll):
                body(Step(c, turn, unroll))
    for c in range(first + turns * unroll, count + lag):
        body(Step(c))


def build(nc, x_in, router_w, router_b, W1, b1, W2, b2, Wq, Wk, Wv, Wo, consts_in, score_decay_in, out):
    ctx = ExitStack()
    with ctx:
        def sb(name, shape, dt=FP32):
            return ctx.enter_context(nc.sbuf_tensor(name, shape, dt))

        def psum(name, width):
            return ctx.enter_context(nc.psum_tensor(name, [TILE, width], FP32))

        def sem(name):
            return ctx.enter_context(nc.semaphore(name))

        def sems(names, suffix):
            return {n: sem(f"{n}_{suffix}") for n in names.split()}

        def ring(name, count):
            return [sem(f"{name}_{i}") for i in range(count)]

        norm_rows = nc.dram_tensor("norm_rows", (ROWS, D), FP32, kind="Internal").ap()
        pick_rows = nc.dram_tensor("pick_rows", (TOP_K * ROWS, D), FP32, kind="Internal").ap()
        slot_rows = nc.dram_tensor("slot_rows", (SLOT_TILES * TILE, D), FP32, kind="Internal").ap()

        x = sb("x_rows", [TILE, ROW_TILES * D])
        consts = sb("consts", [TILE, CONST_WIDTH])
        const = {n: consts[:, a:b] for n, (a, b) in CONST_COLUMNS.items()}
        score_decay = sb("score_decay", [TILE, HEADS * TILE])
        w_q = sb("w_q", [D, D])
        w_kv = sb("w_kv", [D, 2 * D])
        w_o = sb("w_o", [D, D])
        w_router = sb("w_router", [D, TILE])
        bias_router = sb("bias_router", [TILE, EXPERTS])
        w1_high = sb("w1_high", [D, EXPERTS * FF], FP32R)
        w1_low = sb("w1_low", [D, EXPERTS * FF], FP32R)
        w1_raw = sb("w1_raw", [D, EXPERTS * FF])
        w2 = sb("w2", [TILE, EXPERTS * FF_CHUNKS * D])
        bias1 = sb("bias1", [TILE, EXPERTS * FF])
        bias2 = sb("bias2", [TILE, EXPERTS * FF])
        before_bf = sb("before_bf", [TILE, TILE], BF16)
        ones_bf = sb("ones_bf", [TILE, TILE], BF16)
        ones_row = sb("ones_row", [TILE, EXPERTS * ROW_TILES])
        column_bf = sb("column_bf", [TILE, TILE], BF16)

        wait_carrier = sb("wait_carrier", [TILE, 1])
        stats = sb("stats", [TILE, 2, 2, PAIR, 6])
        moments = sb("moments", [TILE, 2, 2, PAIR, 2])
        var_eps = sb("var_eps", [TILE, 2, 2, PAIR])
        inv_var = sb("inv_var", [TILE, 2, 2, PAIR])
        neg_mean = sb("neg_mean", [TILE, 2, 2, PAIR])
        inv_dev = sb("inv_dev", [TILE, 2, 2, PAIR])
        offset_dev = sb("offset_dev", [TILE, 2, 2, PAIR])
        norm = sb("norm", [TILE, 2, 2, PAIR * D])
        norm_t = sb("norm_t", [D, 2, 2, PAIR * TILE])
        logits = sb("logits", [TILE, ROW_TILES, EXPERTS])

        def per_expert(name, dt=FP32):
            return sb(name, [TILE, ROW_TILES, EXPERTS], dt)
        best = sb("best", [TILE, TOP_K, ROW_TILES])
        is_best = per_expert("is_best")
        ranked = per_expert("ranked")
        first_rank = sb("first_rank", [TILE, ROW_TILES])
        pick = [per_expert("pick_0"), per_expert("pick_1")]
        other_logits = per_expert("other_logits")
        picked_bf = per_expert("picked_bf", BF16)
        counts = sb("counts", [TILE, EXPERTS, ROW_TILES])
        running = sb("running", [TILE, EXPERTS * ROW_TILES])
        total = sb("total", [TILE, EXPERTS + 1])
        padded_f = sb("padded_f", [TILE, EXPERTS])
        padded_i = sb("padded_i", [TILE, EXPERTS], I32)
        ends = sb("ends", [TILE, EXPERTS + 1])
        shift = sb("shift", [TILE, EXPERTS])
        place = per_expert("place")
        place_f = sb("place_f", [TILE, TOP_K, ROW_TILES])
        place_i = sb("place_i", [TILE, PICKS], I32)
        place_part_i = sb("place_part_i", [TILE, 2, PICKS], I32)
        place_part = sb("place_part", [TILE, 2, PICKS])
        gap = sb("gap", [TILE, ROW_TILES])
        gap_exp = sb("gap_exp", [TILE, ROW_TILES])
        gap_sum = sb("gap_sum", [TILE, ROW_TILES])
        gate = sb("gate", [TILE, TOP_K, ROW_TILES])
        low_hot = sb("low_hot", [TILE, 2, 4, TILE], BF16)
        high_value = sb("high_value", [TILE, 2, 4, 2 * SLOT_TILES], BF16)
        slot_row_f = sb("slot_row_f", [TILE, SLOT_TILES])
        slot_row_sum = sb("slot_row_sum", [TILE, SLOT_TILES])
        slot_row_i = sb("slot_row_i", [TILE, SLOT_TILES], I32)
        spare = sb("spare", [TILE, SLOT_TILES])
        slot_table = sb("slot_table", [TILE, SLOT_TILES + AHEAD, 2], U32)
        past_end = sb("past_end", [TILE, SLOT_TILES, EXPERTS - 1])
        tile_start = sb("tile_start", [TILE, SLOT_TILES])
        tile_expert_f = sb("tile_expert_f", [TILE, SLOT_TILES])
        expert_offset = sb("expert_offset", [TILE, SLOT_TILES], I32)

        row_index = sb("row_index", [TILE, 4 * 2], U32)
        got = sb("got", [TILE, 4, D])
        got_high = sb("got_high", [D, 2, TILE], FP32R)
        got_low = sb("got_low", [D, 2, TILE], FP32R)
        hidden = sb("hidden", [TILE, 2, FF])
        hidden_t = sb("hidden_t", [TILE, 2, FF])
        result = sb("result", [TILE, 4, D])

        back_index = sb("back_index", [TILE, 2 * PAIR * TOP_K], U32)
        back = sb("back", [TILE, 4, TOP_K, PAIR, D])

        q_blocks = w1_raw[:, :].rearrange("p (u h i) -> p u h i", u=2, h=HEADS)
        k_t = sb("k_t", [D, 2, SEQ_LEN])
        q_later = sb("q_later", [D, 2, TILE])
        k_first = sb("k_first", [TILE, 2, D])
        V_STEP = TILE + HEAD_DIM
        v_blocks = sb("v_blocks", [TILE, 2, PAIR, HEADS * V_STEP])
        state = sb("state", [D, 2, D])
        weights = sb("weights", [TILE, PAIR, HEADS * TILE])
        o_t = sb("o_t", [D, SEQ_LEN])

        def v_diagonal(u, c):
            return v_blocks[:, u, c, :].rearrange("p (h s) -> p h s", s=V_STEP)[:, :, 0:HEAD_DIM]

        bank01, bank23 = psum("bank01", 1024), psum("bank23", 1024)
        bank4, bank5, bank6, bank7 = (psum(f"bank{i}", 512) for i in range(4, 8))
        ps_scores = [bank01, bank23]
        ps_got_t = [bank01[:, 0:TILE], bank01[:, 512:512 + TILE]]
        ps_hidden = [bank23[:, 0:512], bank23[:, 512:1024]]
        ps_hidden_t = [bank4, bank5]
        ps_result = [bank6[:, 0:D], bank7[:, 0:D]]

        consts_loaded, router_loaded, weights_loaded = sem("consts_loaded"), sem("router_loaded"), sem("weights_loaded")
        x_loaded, x_rest_loaded = sem("x_loaded"), sem("x_rest_loaded")
        consts_ready, w1_high_ready, w1_low_ready = sem("consts_ready"), sem("w1_high_ready"), sem("w1_low_ready")
        router_zeroed, table_zeroed, v_zeroed = sem("router_zeroed"), sem("table_zeroed"), sem("v_zeroed")
        w1_loaded = sem("w1_loaded")
        prep = [sems("stats_done moments_done var_ready inv_ready dev_ready offset_ready norm_ready norm_t_ps "
                     "norm_t_ready "
                     "logits_ps logits_ready", f"prep{f}") for f in range(2)]
        rows_stored = [ring(f"rows_stored_prep{f}", 2) for f in range(2)]
        route = [sems("chain picked ranks_ps gap_ready exp_ready hot_ready table_ps rows_ready experts_ready", f"route{f}") for f in range(2)]
        expert = [sems("index_copied got_t_ps high_ready low_ready hidden_ps hidden_ready hidden_t_ps "
                       "hidden_t_ready result_ps result_ready", f"ffn{f}") for f in range(2)]
        gathered = [ring(f"gathered_ffn{f}", 4) for f in range(2)]
        result_stored = [ring(f"result_stored_ffn{f}", 4) for f in range(2)]
        back_gathered, back_loaded = ring("back_gathered", 2), ring("back_loaded", 4)
        comb = [sems("index_copied first_added added", f"back{f}") for f in range(2)]
        att = sems("stats_done moments_done var_ready inv_ready dev_ready offset_ready norm_ready norm_t_ps "
                   "norm_t_ready qkv_ps k_ready kv_ready q_later_ready state_ps state_ready scores_ps0 scores_ps1 weights_ready0 "
                   "weights_ready1 o_ps o_ready proj_ps x_ready", "att")
        out_stored = ring("out_stored", 2)

        SCORES_PS = [att["scores_ps0"], att["scores_ps1"]]
        WEIGHTS_READY = [att["weights_ready0"], att["weights_ready1"]]

        def x_pair(step):
            return x[:, bass.ds(step.n * (PAIR * D), PAIR * D)]

        block = ctx.enter_context(nc.Block())

        @block.sync
        def _(sp):
            def rows_of(a, b):
                return x_in[a:b, :, :].rearrange("b (t p) d -> p (b t) d", p=TILE)

            sp.dma_start(x[:, 0:4 * PAIR * D].rearrange("p (t d) -> p t d", d=D), rows_of(0, 4)).then_inc(x_loaded, 16)
            sp.dma_start(x[:, 4 * PAIR * D:].rearrange("p (t d) -> p t d", d=D), rows_of(4, SEQS))\
              .then_inc(x_rest_loaded, 16)
            sp.dma_start(w1_raw[:, :].rearrange("p (e f) -> p e f", e=EXPERTS), W1.rearrange("e p f -> p e f"))\
              .then_inc(w1_loaded, 16)
            sp.dma_start(w2[:, :].rearrange("p (e c d) -> p e c d", e=EXPERTS, c=FF_CHUNKS),
                         W2.rearrange("e (c p) d -> p e c d", p=TILE)).then_inc(weights_loaded, 16)
            sp.dma_start(bias1[:, :], b1.rearrange("e f -> (e f)").partition_broadcast(TILE))\
              .then_inc(weights_loaded, 16)
            sp.dma_start(bias2[:, :].rearrange("p (e f) -> p e f", e=EXPERTS)[:, :, 0:D],
                         b2.rearrange("e d -> (e d)").partition_broadcast(TILE)
                           .rearrange("p (e d) -> p e d", e=EXPERTS)).then_inc(weights_loaded, 16)
            for w, source in ((w_q[:, :], Wq), (w_kv[:, 0:D], Wk), (w_kv[:, D:2 * D], Wv), (w_o[:, :], Wo),
                              (score_decay[:, :], score_decay_in)):
                sp.dma_start(w, source).then_inc(weights_loaded, 16)

            def store_norm(f, b, which):
                wait_step(sp, prep[f]["norm_ready"], b)
                sp.dma_start(norm_rows[bass.ds(b.n * (PAIR * TILE), PAIR * TILE), :]
                             .rearrange("(t p) d -> p t d", p=TILE),
                             norm[:, which, b.slot(2), :].rearrange("p (t d) -> p t d", d=D))\
                  .then_inc(rows_stored[f][b.slot(2)], 16)

            def store_result(f, j):
                wait_step(sp, expert[f]["result_ready"], j)
                sp.dma_start(slot_rows[bass.ds(j.n * TILE, TILE), :], result[:, j.slot(4), :])\
                  .then_inc(result_stored[f][j.slot(4)], 16)

            def load_back(b):
                wait_step(sp, comb[1]["added"], b.after(-4), PAIR)
                for k in range(TOP_K):
                    sp.dma_start(back[:, b.slot(4), k, :, :],
                                 pick_rows.rearrange("(k t p) d -> k p t d", k=TOP_K, p=TILE)
                                 [k][:, bass.ds(b.n * PAIR, PAIR), :]).then_inc(back_loaded[b.slot(4)], 16)

            def store_out(b):
                wait_step(sp, comb[1]["added"], b, PAIR)
                sp.dma_start(out[bass.ds(b.n, 1), :, :].rearrange("b (t p) d -> p (b t) d", p=TILE),
                             x_pair(b).rearrange("p (t d) -> p t d", d=D)).then_inc(out_stored[b.slot(2)], 16)

            def last_step(b):
                if b.after(3).within(PAIRS):
                    load_back(b.after(3))
                if b.within(PAIRS):
                    store_out(b)

            run_steps(sp, PAIRS, 2, 0, 0, lambda b: store_norm(0, b, 1))
            run_steps(sp, SLOT_TILES, 4, 0, 0, lambda j: store_result(0, j))
            run_steps(sp, PAIRS, 2, 0, 0, lambda b: store_norm(1, b, 1))
            for s in range(4):
                sp.wait_ge(result_stored[1][s], SLOT_TILES // 4 * 16)
            run_steps(sp, PAIRS, 4, 0, 3, last_step)
            for s in range(2):
                sp.wait_ge(out_stored[s], PAIRS // 2 * 16)

        @block.gpsimd
        def _(pool):
            nc.gpsimd.memset(slot_table[:, :, :].rearrange("p j c -> p (j c)"), 0).then_inc(table_zeroed, 1)
            nc.gpsimd.memset(v_blocks[:, :, :, :].rearrange("p a b c -> p (a b c)"), 0.0).then_inc(v_zeroed, 1)
            pool.wait_ge(w1_high_ready, 1)
            nc.gpsimd.tensor_tensor(w1_low[:, :], w1_raw[:, :], w1_high[:, :].bitcast(FP32), ALU.subtract)\
              .then_inc(w1_low_ready, 1)

            def copy_row_index(f, j):
                nc.gpsimd.tensor_copy(row_index[:, j.slot(4) * 2:j.slot(4) * 2 + 2],
                                      slot_table[:, bass.ds(j.n, 1), :].rearrange("p a c -> p (a c)"))\
                  .then_inc(expert[f]["index_copied"], 1)

            def gather_tile(f, j):
                n = j.slot(4) * 2
                nc.gpsimd.indirect_dma_start(
                    out=got[:, j.slot(4), :], out_offset=None, in_=norm_rows,
                    in_offset=bass.IndirectOffsetOnAxis(ap=row_index[:, n:n + 1], axis=0))\
                  .then_inc(gathered[f][j.slot(4)], 16)

            def gather_step(j):
                wait_step(pool, expert[0]["index_copied"], j)
                wait_step(pool, expert[0]["got_t_ps"], j.after(-4))
                if j.after(1).within(SLOT_TILES):
                    wait_slot(pool, gathered[0], j.after(1 - 4))
                    copy_row_index(0, j.after(1))
                gather_tile(0, j)

            def gather_scatter_step(j):
                done = j.after(-AHEAD)
                wait_step(pool, expert[1]["index_copied"], j)
                if j.within(SLOT_TILES):
                    wait_step(pool, expert[1]["got_t_ps"], j.after(-4))
                if done.within(SLOT_TILES):
                    wait_step(pool, expert[1]["result_ready"], done)
                if j.after(1).within(SLOT_TILES + AHEAD):
                    if j.after(1 - 4).within(SLOT_TILES):
                        wait_slot(pool, gathered[1], j.after(1 - 4))
                    wait_slot(pool, result_stored[1], done.after(1 - 4))
                    copy_row_index(1, j.after(1))
                if j.within(SLOT_TILES):
                    gather_tile(1, j)
                if done.within(SLOT_TILES):
                    n = j.slot(4) * 2 + 1
                    nc.gpsimd.indirect_dma_start(
                        out=pick_rows, out_offset=bass.IndirectOffsetOnAxis(ap=row_index[:, n:n + 1], axis=0),
                        in_=result[:, done.slot(4), :], in_offset=None, bounds_check=TOP_K * ROWS - 1,
                        oob_is_err=False).then_inc(result_stored[1][done.slot(4)], 16)

            def copy_back_index(b):
                u = b.slot(2)
                nc.gpsimd.tensor_copy(
                    back_index[:, u * 4:u * 4 + 4].rearrange("p (k t) -> p k t", k=TOP_K),
                    place_i[:, :].bitcast(U32).rearrange("p (k t) -> p k t", k=TOP_K)
                    [:, :, bass.ds(b.n * PAIR, PAIR)]).then_inc(comb[0]["index_copied"], 1)

            def gather_back(b):
                u = b.slot(2)
                wait_step(pool, comb[0]["index_copied"], b)
                wait_step(pool, comb[0]["added"], b.after(-2), PAIR)
                if b.after(1).within(PAIRS):
                    wait_slot(pool, back_gathered, b.after(1 - 2), 16 * 4)
                    copy_back_index(b.after(1))
                for k in range(TOP_K):
                    for t in range(PAIR):
                        n = u * 4 + k * PAIR + t
                        nc.gpsimd.indirect_dma_start(
                            out=back[:, u, k, t, :], out_offset=None, in_=slot_rows,
                            in_offset=bass.IndirectOffsetOnAxis(ap=back_index[:, n:n + 1], axis=0))\
                          .then_inc(back_gathered[u], 16)

            def table_and_rows(f):
                pool.wait_ge(route[f]["rows_ready"], 1)
                for s in range(2):
                    pool.wait_ge(rows_stored[f][s], PAIRS // 2 * 16)

            table_and_rows(0)
            copy_row_index(0, Step(0))
            run_steps(pool, SLOT_TILES, 4, 0, 0, gather_step, tail=1)
            for s in range(4):
                pool.wait_ge(result_stored[0][s], SLOT_TILES // 4 * 16)
            copy_back_index(Step(0))
            run_steps(pool, PAIRS, 2, 0, 0, gather_back, tail=1)
            table_and_rows(1)
            copy_row_index(1, Step(0))
            run_steps(pool, SLOT_TILES, 4, 8, 0, lambda j: gather_scatter_step(j)
                      if j.within(SLOT_TILES + AHEAD) else None)

        @block.scalar
        def _(act):
            act.dma_start(consts[:, :], consts_in).then_inc(consts_loaded, 16)
            act.wait_ge(router_zeroed, 1)
            act.dma_start(w_router[:, 0:EXPERTS], router_w).then_inc(router_loaded, 16)
            act.dma_start(bias_router[:, :], router_b.partition_broadcast(TILE)).then_inc(router_loaded, 16)

            def normalise(s, b, which, reader, stored=None):
                u = b.slot(2)
                wait_step(act, s["inv_ready"], b)
                nc.scalar.activation(inv_dev[:, which, u, :], inv_var[:, which, u, :], ACT.Sqrt)\
                  .then_inc(s["dev_ready"], 1)
                wait_step(act, s["dev_ready"], b)
                for t in range(PAIR):
                    last = nc.scalar.activation(offset_dev[:, which, u, t:t + 1], neg_mean[:, which, u, t:t + 1],
                                                ACT.Copy, scale=inv_dev[:, which, u, t:t + 1])
                last.then_inc(s["offset_ready"], 1)
                wait_step(act, s["offset_ready"], b)
                wait_step(act, reader, b.after(-2))
                if stored is not None:
                    wait_slot(act, stored, b.after(-2))
                for t in range(PAIR):
                    last = nc.scalar.activation(norm[:, which, u, t * D:(t + 1) * D],
                                                x[:, bass.ds((b.n * PAIR + t) * D, D)], ACT.Identity,
                                                bias=offset_dev[:, which, u, t:t + 1],
                                                scale=inv_dev[:, which, u, t:t + 1])
                last.then_inc(s["norm_ready"], 1)

            def copy_norm_t(s, b, which, ps, readers):
                wait_step(act, s["norm_t_ps"], b)
                wait_step(act, readers, b.after(-2))
                nc.scalar.activation(norm_t[:, which, b.slot(2), :], ps, ACT.Copy)\
                  .then_inc(s["norm_t_ready"], 1)

            def first_prep(b):
                if b.after(1).within(PAIRS):
                    normalise(prep[0], b.after(1), 1, prep[0]["norm_t_ps"], rows_stored[0])
                if b.within(PAIRS):
                    copy_norm_t(prep[0], b, 1, (bank6, bank7)[b.slot(2)][:, 0:SEQ_LEN], prep[0]["logits_ps"])

            def exp_gap(f):
                act.wait_ge(route[f]["gap_ready"], 1)
                nc.scalar.activation(gap_exp[:, :], gap[:, :], ACT.Exp).then_inc(route[f]["exp_ready"], 1)

            def split_high(f, j):
                wait_step(act, expert[f]["got_t_ps"], j)
                wait_step(act, expert[f]["hidden_ps"], j.after(-2))
                nc.scalar.activation(got_high[:, j.slot(2), :], ps_got_t[j.slot(2)], ACT.Copy)\
                  .then_inc(expert[f]["high_ready"], 1)

            def relu_tile(f, j):
                wait_step(act, expert[f]["hidden_t_ps"], j)
                wait_step(act, expert[f]["result_ps"], j.after(-2))
                nc.scalar.activation(hidden_t[:, j.slot(2), :], ps_hidden_t[j.slot(2)][:, :], ACT.Relu)\
                  .then_inc(expert[f]["hidden_t_ready"], 1)

            def expert_step(f, s):
                if s.after(1).within(SLOT_TILES):
                    relu_tile(f, s.after(1))
                if s.after(4).within(SLOT_TILES):
                    split_high(f, s.after(4))

            def copy_queries(b):
                u = b.slot(2)
                wait_step(act, att["qkv_ps"], b)
                wait_step(act, SCORES_PS[1], b.after(-2))
                for h in range(HEADS):
                    nc.scalar.activation(q_blocks[:, u, h, :], bank4[:, 0:SEQ_LEN], ACT.Copy,
                                         scale=const["head_rows"][:, h:h + 1])
                nc.scalar.activation(k_t[:, u, :], bank4[:, SEQ_LEN:2 * SEQ_LEN], ACT.Copy)\
                  .then_inc(att["k_ready"], 1)

            def copy_o(b):
                wait_step(act, att["o_ps"], b)
                wait_step(act, att["proj_ps"], b.after(-1))
                nc.scalar.activation(o_t[:, :], bank7[:, 0:SEQ_LEN], ACT.Copy).then_inc(att["o_ready"], 1)

            def middle(s):
                if s.after(1).within(PAIRS):
                    copy_norm_t(att, s.after(1), 0, bank6[:, 0:SEQ_LEN], att["qkv_ps"])
                    copy_queries(s.after(1))
                if s.after(2).within(PAIRS):
                    normalise(att, s.after(2), 0, att["norm_t_ps"])
                if s.within(PAIRS):
                    copy_o(s)
                if s.after(-2).within(PAIRS):
                    copy_norm_t(prep[1], s.after(-2), 1, bank6[:, SEQ_LEN:2 * SEQ_LEN], prep[1]["logits_ps"])
                if s.after(-1).within(PAIRS):
                    normalise(prep[1], s.after(-1), 1, prep[1]["norm_t_ps"], rows_stored[1])

            run_steps(act, PAIRS, 2, 0, 1, first_prep)
            act.wait_ge(w1_loaded, 16)
            nc.scalar.activation(w1_high[:, :], w1_raw[:, :], ACT.Copy).then_inc(w1_high_ready, 1)
            exp_gap(0)
            run_steps(act, SLOT_TILES, 4, 0, 4, lambda s: expert_step(0, s))
            act.wait_ge(w1_low_ready, 1)
            run_steps(act, PAIRS, 2, 2, 2, middle)
            exp_gap(1)
            run_steps(act, SLOT_TILES, 4, 0, 4, lambda s: expert_step(1, s))

        @block.vector
        def _(dve):
            nc.vector.memset(w_router[:, :], 0.0).then_inc(router_zeroed, 1)
            nc.vector.memset(ones_bf[:, :], 1.0)
            nc.vector.memset(ones_row[:, :], 1.0)
            nc.vector.memset(total[:, 0:1], 0.0)
            nc.vector.memset(ends[:, 0:1], 0.0)
            dve.wait_ge(consts_loaded, 16)
            nc.vector.tensor_copy(before_bf[:, :], const["before"])
            nc.vector.tensor_copy(column_bf[:, :], const["column"])
            nc.vector.tensor_scalar(tile_start[:, :], const["column"][:, 0:SLOT_TILES], float(TILE), None, ALU.mult)\
              .then_inc(consts_ready, 1)

            def carry_wait():
                nc.vector.memset(wait_carrier[:, :], 0.0)

            def take_stats(s, b, which):
                u = b.slot(2)
                carry_wait()
                for t in range(PAIR):
                    last = nc.vector.bn_stats(stats[:, which, u, t, :], x[:, bass.ds((b.n * PAIR + t) * D, D)])
                last.then_inc(s["stats_done"], 1)
                wait_step(dve, s["stats_done"], b)
                carry_wait()
                for t in range(PAIR):
                    last = nc.vector.bn_aggr(moments[:, which, u, t, :], stats[:, which, u, t, :])
                last.then_inc(s["moments_done"], 1)
                wait_step(dve, s["moments_done"], b)
                nc.vector.tensor_scalar(var_eps[:, which, u, :], moments[:, which, u, :, 1], EPS, None, ALU.add)\
                  .then_inc(s["var_ready"], 1)
                wait_step(dve, s["norm_ready"], b.after(-2))
                nc.vector.tensor_scalar(neg_mean[:, which, u, :], moments[:, which, u, :, 0], -1.0, None, ALU.mult)
                wait_step(dve, s["var_ready"], b)
                nc.vector.reciprocal(inv_var[:, which, u, :], var_eps[:, which, u, :]).then_inc(s["inv_ready"], 1)

            def add_router_bias(s, b, ps):
                wait_step(dve, s["logits_ps"], b)
                nc.vector.tensor_tensor(
                    logits[:, bass.ds(b.n * PAIR, PAIR), :],
                    ps.rearrange("p (t c) -> p t c", t=PAIR)[:, :, 0:EXPERTS],
                    bias_router[:, :].unsqueeze(1).to_broadcast([TILE, PAIR, EXPERTS]), ALU.add)\
                  .then_inc(s["logits_ready"], 1)

            def first_prep(b):
                if b.turn is None and b.c + 2 == 4:
                    dve.wait_ge(x_rest_loaded, 16)
                if b.after(2).within(PAIRS):
                    take_stats(prep[0], b.after(2), 1)
                if b.after(-1).within(PAIRS):
                    add_router_bias(prep[0], b.after(-1),
                                    (bank6, bank7)[b.after(-1).slot(2)][:, SEQ_LEN:2 * SEQ_LEN])

            def route_rows(f):
                r = route[f]
                done = [0]

                def link(ins):
                    done[0] += 1
                    ins.then_inc(r["chain"], 1)
                    dve.wait_ge(r["chain"], done[0])

                def over_experts(a):
                    return a.unsqueeze(2).to_broadcast([TILE, ROW_TILES, EXPERTS])

                rank = const["low_first"].unsqueeze(1).to_broadcast([TILE, ROW_TILES, EXPERTS])
                scores = logits
                for k in range(TOP_K):
                    link(nc.vector.tensor_reduce(best[:, k, :], scores[:, :, :], AXX, ALU.max))
                    link(nc.vector.tensor_tensor(is_best[:, :, :], scores[:, :, :], over_experts(best[:, k, :]),
                                                 ALU.is_equal))
                    link(nc.vector.tensor_tensor(ranked[:, :, :], is_best[:, :, :], rank, ALU.mult))
                    link(nc.vector.tensor_reduce(first_rank[:, :], ranked[:, :, :], AXX, ALU.max))
                    link(nc.vector.tensor_tensor(pick[k][:, :, :], over_experts(first_rank[:, :]), rank,
                                                 ALU.is_equal))
                    if k == 0:
                        link(nc.vector.scalar_tensor_tensor(other_logits[:, :, :], pick[0][:, :, :], FAR_BELOW,
                                                            logits[:, :, :], ALU.mult, ALU.add))
                        scores = other_logits
                nc.vector.tensor_tensor(picked_bf[:, :, :], pick[0][:, :, :], pick[1][:, :, :], ALU.add)\
                  .then_inc(r["picked"], 1)
                nc.vector.tensor_tensor(gap[:, :], best[:, 1, :], best[:, 0, :], ALU.subtract)\
                  .then_inc(r["gap_ready"], 1)
                dve.wait_ge(r["ranks_ps"], 1)
                link(nc.vector.tensor_copy(counts[:, :, :],
                                           bank4[:, 256:512].rearrange("p (t e) -> p e t", e=EXPERTS)))
                link(nc.vector.tensor_tensor_scan(running[:, :], ones_row[:, :],
                                                  counts[:, :, :].rearrange("p e t -> p (e t)"), 0.0,
                                                  ALU.mult, ALU.add))
                running_e = running[:, :].rearrange("p (e t) -> p e t", e=EXPERTS)
                nc.vector.tensor_copy(total[:, 1:EXPERTS + 1], running_e[:, :, ROW_TILES - 1])
                link(nc.vector.tensor_tensor(counts[:, :, :], running_e, counts[:, :, :], ALU.subtract))
                link(nc.vector.scalar_tensor_tensor(padded_i[:, :], total[:, 1:EXPERTS + 1], float(TILE - 1),
                                                    total[:, 0:EXPERTS], ALU.add, ALU.subtract))
                link(nc.vector.tensor_scalar(padded_i[:, :], padded_i[:, :], -TILE, None, ALU.bitwise_and))
                link(nc.vector.tensor_copy(padded_f[:, :], padded_i[:, :]))
                link(nc.vector.tensor_tensor_scan(ends[:, 1:EXPERTS + 1], ones_row[:, 0:EXPERTS], padded_f[:, :],
                                                  0.0, ALU.mult, ALU.add))
                link(nc.vector.tensor_tensor(shift[:, :], ends[:, 0:EXPERTS], total[:, 0:EXPERTS], ALU.subtract))
                link(nc.vector.tensor_tensor(counts[:, :, :], counts[:, :, :],
                                             shift[:, :].unsqueeze(2).to_broadcast([TILE, EXPERTS, ROW_TILES]),
                                             ALU.add))
                link(nc.vector.tensor_tensor(place[:, :, :],
                                             bank4[:, 0:256].rearrange("p (t e) -> p t e", e=EXPERTS),
                                             counts[:, :, :].rearrange("p e t -> p t e"), ALU.add))
                for k in range(TOP_K):
                    link(nc.vector.tensor_tensor(ranked[:, :, :], pick[k][:, :, :], place[:, :, :], ALU.mult))
                    link(nc.vector.tensor_reduce(place_f[:, k, :], ranked[:, :, :], AXX, ALU.add))
                link(nc.vector.tensor_copy(place_i[:, :], place_f[:, :, :].rearrange("p k t -> p (k t)")))
                nc.vector.tensor_scalar(place_part_i[:, 0, :], place_i[:, :], TILE - 1, None, ALU.bitwise_and)
                link(nc.vector.tensor_scalar(place_part_i[:, 1, :], place_i[:, :], TILE.bit_length() - 1, None,
                                             ALU.logical_shift_right))
                link(nc.vector.tensor_copy(place_part[:, :, :], place_part_i[:, :, :]))

                def hot_group(g):
                    u = g.slot(2)
                    wait_step(dve, r["table_ps"], g.after(-2))
                    for i in range(4):
                        column = bass.ds(g.n * 4 + i, 1)
                        nc.vector.tensor_scalar(low_hot[:, u, i, :], column_bf[:, :], place_part[:, 0, column], None,
                                                ALU.is_equal)
                        nc.vector.tensor_scalar(high_value[:, u, i, 0:SLOT_TILES], column_bf[:, 0:SLOT_TILES],
                                                place_part[:, 1, column], const["tile_base"][:, column],
                                                ALU.is_equal, ALU.mult)
                        last = nc.vector.tensor_scalar(high_value[:, u, i, SLOT_TILES:2 * SLOT_TILES],
                                                       column_bf[:, 0:SLOT_TILES], place_part[:, 1, column],
                                                       const["partition"], ALU.is_equal, ALU.mult)
                    last.then_inc(r["hot_ready"], 1)

                run_steps(dve, PICKS // 4, 2, 0, 0, hot_group)
                dve.wait_ge(table_zeroed, 1)
                dve.wait_ge(r["table_ps"], PICKS // 4)
                link(nc.vector.tensor_copy(slot_row_f[:, :], bank5[:, 0:SLOT_TILES]))
                link(nc.vector.tensor_tensor(slot_row_sum[:, :], slot_row_f[:, :],
                                             bank5[:, SLOT_TILES:2 * SLOT_TILES], ALU.add))
                link(nc.vector.tensor_scalar(slot_row_i[:, :], slot_row_sum[:, :], -1.0, 0.0, ALU.add, ALU.max))
                if f == 1:
                    link(nc.vector.tensor_scalar(spare[:, :], slot_row_sum[:, :], 0.0, NOWHERE, ALU.is_equal,
                                                 ALU.mult))
                    nc.vector.scalar_tensor_tensor(slot_table[:, AHEAD:, 1], slot_row_sum[:, :], -1.0, spare[:, :],
                                                   ALU.add, ALU.add)
                nc.vector.tensor_scalar(slot_table[:, 0:SLOT_TILES, 0].bitcast(I32), slot_row_i[:, :], ROWS - 1, None,
                                        ALU.bitwise_and).then_inc(r["rows_ready"], 1)
                link(nc.vector.tensor_tensor(
                    past_end[:, :, :], tile_start[:, :].unsqueeze(2).to_broadcast([TILE, SLOT_TILES, EXPERTS - 1]),
                    ends[:, 1:EXPERTS].unsqueeze(1).to_broadcast([TILE, SLOT_TILES, EXPERTS - 1]), ALU.is_ge))
                link(nc.vector.tensor_reduce(tile_expert_f[:, :], past_end[:, :, :], AXX, ALU.add))
                nc.vector.tensor_scalar(expert_offset[:, :], tile_expert_f[:, :], float(FF), None, ALU.mult)\
                  .then_inc(r["experts_ready"], 1)
                dve.wait_ge(r["exp_ready"], 1)
                link(nc.vector.tensor_scalar(gap_sum[:, :], gap_exp[:, :], 2.0, 2.0, ALU.mult, ALU.add))
                link(nc.vector.reciprocal(gate[:, 0, :], gap_sum[:, :]))
                link(nc.vector.tensor_tensor(gate[:, 1, :], gate[:, 0, :], gap_exp[:, :], ALU.mult))

            offsets = {}

            def load_offsets(first, count):
                _, values = nc.values_load_multi_w_load_instructions(
                    expert_offset[0:1, bass.ds(first.n, count)], engines=[mybir.EngineType.DVE], min_val=0,
                    max_val=(EXPERTS - 1) * FF,
                    skip_runtime_bounds_check_because="a sum of EXPERTS - 1 comparisons times FF")
                for i in range(count):
                    offsets[first.turn is None, first.c + i] = values[i]

            def offset(j):
                key = (j.turn is None, j.c)
                if key not in offsets:
                    load_offsets(j, 1)
                return offsets[key]

            def add_bias1(f, j):
                at = offset(j)
                wait_step(dve, expert[f]["hidden_ps"], j)
                wait_step(dve, expert[f]["hidden_t_ps"], j.after(-2))
                nc.vector.tensor_tensor(hidden[:, j.slot(2), :], ps_hidden[j.slot(2)], bias1[:, bass.ds(at, FF)],
                                        ALU.add).then_inc(expert[f]["hidden_ready"], 1)

            def add_bias2(f, j):
                at = offset(j)
                wait_step(dve, expert[f]["result_ps"], j)
                wait_slot(dve, result_stored[f], j.after(-4))
                nc.vector.tensor_tensor(result[:, j.slot(4), :], ps_result[j.slot(2)], bias2[:, bass.ds(at, D)],
                                        ALU.add).then_inc(expert[f]["result_ready"], 1)

            def split_low(f, j):
                wait_step(dve, expert[f]["high_ready"], j)
                wait_step(dve, expert[f]["hidden_ps"], j.after(-2))
                nc.vector.tensor_tensor(got_low[:, j.slot(2), :], ps_got_t[j.slot(2)],
                                        got_high[:, j.slot(2), :].bitcast(FP32), ALU.subtract)\
                  .then_inc(expert[f]["low_ready"], 1)

            def expert_step(f, s):
                if s.after(2).within(SLOT_TILES):
                    add_bias1(f, s.after(2))
                if s.within(SLOT_TILES):
                    add_bias2(f, s)
                if s.after(4).within(SLOT_TILES):
                    split_low(f, s.after(4))

            def run_experts(f):
                offsets.clear()
                run_steps(dve, SLOT_TILES, 4, 0, 4, lambda s: expert_step(f, s),
                          group=lambda first: load_offsets(first, 6))

            def add_back(f, b):
                u = b.slot(2) if f == 0 else b.slot(4)
                if f == 0:
                    wait_slot(dve, back_gathered, b, 16 * 4)
                else:
                    wait_slot(dve, back_loaded, b, 16 * TOP_K)
                for k in range(TOP_K):
                    if k:
                        wait_step(dve, comb[f]["first_added"], b, PAIR)
                    for t in range(PAIR):
                        row = x[:, bass.ds((b.n * PAIR + t) * D, D)]
                        nc.vector.scalar_tensor_tensor(row, back[:, u, k, t, :],
                                                       gate[:, k, bass.ds(b.n * PAIR + t, 1)], row,
                                                       ALU.mult, ALU.add)\
                          .then_inc(comb[f]["added" if k else "first_added"], 1)

            def weigh_scores(b, c):
                wait_step(dve, SCORES_PS[c], b)
                wait_step(dve, att["o_ps"], b.after(-1))
                nc.vector.tensor_tensor(weights[:, c, :], ps_scores[c][:, :], score_decay[:, :], ALU.mult)\
                  .then_inc(WEIGHTS_READY[c], 1)

            def copy_keys_values(b):
                u = b.slot(2)
                wait_step(dve, att["qkv_ps"], b)
                wait_step(dve, att["o_ps"], b.after(-2))
                nc.vector.tensor_tensor(k_first[:, u, :], bank5[:, 0:D], const["key_decay"], ALU.mult)
                for c in range(PAIR):
                    last = nc.vector.tensor_copy(v_diagonal(u, c), bank5[:, D * (1 + c):D * (2 + c)]
                                                 .rearrange("p (h e) -> p h e", h=HEADS))
                last.then_inc(att["kv_ready"], 1)

            def decay_queries(b):
                wait_step(dve, att["k_ready"], b)
                nc.vector.tensor_tensor(q_later[:, b.slot(2), :], bank4[:, TILE:SEQ_LEN], const["query_decay"],
                                        ALU.mult).then_inc(att["q_later_ready"], 1)

            def mask_state(b):
                wait_step(dve, att["state_ps"], b)
                nc.vector.tensor_tensor(state[:, b.slot(2), :], bank5[:, 3 * D:4 * D], const["same_head"], ALU.mult)\
                  .then_inc(att["state_ready"], 1)

            def add_projection(b):
                wait_step(dve, att["proj_ps"], b)
                nc.vector.tensor_tensor(x_pair(b), x_pair(b), bank7[:, SEQ_LEN:2 * SEQ_LEN], ALU.add)\
                  .then_inc(att["x_ready"], 1)

            def middle(s):
                if s.within(PAIRS):
                    weigh_scores(s, 1)
                if s.after(2).within(PAIRS):
                    add_back(0, s.after(2))
                    wait_step(dve, comb[0]["added"], s.after(2), PAIR)
                    take_stats(att, s.after(2), 0)
                if s.after(1).within(PAIRS):
                    copy_keys_values(s.after(1))
                    decay_queries(s.after(1))
                    mask_state(s.after(1))
                    weigh_scores(s.after(1), 0)
                if s.within(PAIRS):
                    add_projection(s)
                if s.after(-2).within(PAIRS):
                    add_router_bias(prep[1], s.after(-2), bank6[:, SEQ_LEN:2 * SEQ_LEN])
                if s.within(PAIRS):
                    wait_step(dve, att["x_ready"], s)
                    take_stats(prep[1], s, 1)

            dve.wait_ge(x_loaded, 16)
            run_steps(dve, PAIRS, 2, 1, 2, first_prep)
            dve.wait_ge(prep[0]["logits_ready"], PAIRS)
            route_rows(0)
            dve.wait_ge(route[0]["experts_ready"], 1)
            dve.wait_ge(weights_loaded, 16 * 8)
            dve.wait_ge(v_zeroed, 1)
            run_experts(0)
            run_steps(dve, PAIRS, 2, 2, 2, middle)
            dve.wait_ge(prep[1]["logits_ready"], PAIRS)
            route_rows(1)
            dve.wait_ge(route[1]["experts_ready"], 1)
            run_experts(1)
            run_steps(dve, PAIRS, 4, 0, 0, lambda b: add_back(1, b))

        @block.tensor
        def _(pe):
            identity = const["identity"]

            def transpose_norm(s, b, which, ps):
                wait_step(pe, s["norm_ready"], b)
                for t in range(PAIR):
                    last = nc.tensor.transpose(ps[:, t * TILE:(t + 1) * TILE],
                                               norm[:, which, b.slot(2), t * D:(t + 1) * D], identity)
                last.then_inc(s["norm_t_ps"], 1)

            def router(s, b, ps):
                wait_step(pe, s["norm_t_ready"], b)
                for t in range(PAIR):
                    last = nc.tensor.matmul(ps[:, t * TILE:(t + 1) * TILE],
                                            norm_t[:, 1, b.slot(2), t * TILE:(t + 1) * TILE], w_router[:, :],
                                            start=True, stop=True)
                last.then_inc(s["logits_ps"], 1)

            def first_prep(s):
                b = s.after(1)
                if b.within(PAIRS):
                    wait_step(pe, prep[0]["logits_ready"], b.after(-2))
                    transpose_norm(prep[0], b, 1, (bank6, bank7)[b.slot(2)][:, 0:SEQ_LEN])
                if s.within(PAIRS):
                    router(prep[0], s, (bank6, bank7)[s.slot(2)][:, SEQ_LEN:2 * SEQ_LEN])

            def route_rows(f):
                r = route[f]
                pe.wait_ge(r["picked"], 1)
                flat = picked_bf[:, :, :].rearrange("p t e -> p (t e)")
                nc.tensor.matmul(bank4[:, 0:256], before_bf[:, :], flat, start=True, stop=True)
                nc.tensor.matmul(bank4[:, 256:512], ones_bf[:, :], flat, start=True, stop=True)\
                  .then_inc(r["ranks_ps"], 1)

                def table_group(g):
                    u = g.slot(2)
                    wait_step(pe, r["hot_ready"], g)
                    for i in range(4):
                        last = nc.tensor.matmul(bank5[:, 0:2 * SLOT_TILES], low_hot[:, u, i, :],
                                                high_value[:, u, i, :],
                                                start=g.turn is None and g.c == 0 and i == 0,
                                                stop=g.turn is None and g.c == PICKS // 4 - 1 and i == 3)
                    last.then_inc(r["table_ps"], 1)

                run_steps(pe, PICKS // 4, 2, 0, 0, table_group, tail=2)

            offsets = {}

            def load_offsets(first, count):
                _, values = nc.values_load_multi_w_load_instructions(
                    expert_offset[0:1, bass.ds(first.n, count)], engines=[mybir.EngineType.PE], min_val=0,
                    max_val=(EXPERTS - 1) * FF,
                    skip_runtime_bounds_check_because="a sum of EXPERTS - 1 comparisons times FF")
                for i in range(count):
                    offsets[first.turn is None, first.c + i] = values[i]

            def offset(j):
                key = (j.turn is None, j.c)
                if key not in offsets:
                    load_offsets(j, 1)
                return offsets[key]

            def transpose_got(f, j):
                wait_slot(pe, gathered[f], j)
                wait_step(pe, expert[f]["low_ready"], j.after(-2))
                nc.tensor.transpose(ps_got_t[j.slot(2)], got[:, j.slot(4), :], identity)\
                  .then_inc(expert[f]["got_t_ps"], 1)

            def first_product(f, j):
                at, u = offset(j), j.slot(2)
                wait_step(pe, expert[f]["low_ready"], j)
                wait_step(pe, expert[f]["hidden_ready"], j.after(-2))
                parts = ((got_high, w1_high), (got_high, w1_low), (got_low, w1_high))
                for n, (rows, w) in enumerate(parts):
                    last = nc.tensor.matmul(ps_hidden[u], rows[:, u, :], w[:, bass.ds(at, FF)],
                                            start=n == 0, stop=n == len(parts) - 1)
                last.then_inc(expert[f]["hidden_ps"], 1)

            def transpose_hidden(f, j):
                u = j.slot(2)
                wait_step(pe, expert[f]["hidden_ready"], j)
                wait_step(pe, expert[f]["hidden_t_ready"], j.after(-2))
                for c in range(FF_CHUNKS):
                    last = nc.tensor.transpose(ps_hidden_t[u][:, c * TILE:(c + 1) * TILE],
                                               hidden[:, u, c * TILE:(c + 1) * TILE], identity)
                last.then_inc(expert[f]["hidden_t_ps"], 1)

            def second_product(f, j):
                at, u = offset(j), j.slot(2)
                wait_step(pe, expert[f]["hidden_t_ready"], j)
                wait_step(pe, expert[f]["result_ready"], j.after(-2))
                for c in range(FF_CHUNKS):
                    last = nc.tensor.matmul(ps_result[u], hidden_t[:, u, c * TILE:(c + 1) * TILE],
                                            w2[:, bass.ds(at + c * D, D)], start=c == 0, stop=c == FF_CHUNKS - 1)
                last.then_inc(expert[f]["result_ps"], 1)

            def expert_step(f, s):
                if s.after(2).within(SLOT_TILES):
                    first_product(f, s.after(2))
                if s.after(1).within(SLOT_TILES):
                    transpose_hidden(f, s.after(1))
                if s.within(SLOT_TILES):
                    second_product(f, s)
                if s.after(4).within(SLOT_TILES):
                    transpose_got(f, s.after(4))

            def run_experts(f):
                pe.wait_ge(route[f]["experts_ready"], 1)
                offsets.clear()
                run_steps(pe, SLOT_TILES, 4, 0, 4, lambda s: expert_step(f, s),
                          group=lambda first: load_offsets(first, 6))

            def project(b):
                u = b.slot(2)
                wait_step(pe, att["norm_t_ready"], b)
                wait_step(pe, att["state_ready"], b.after(-1))
                xt = norm_t[:, 0, u, :]
                nc.tensor.matmul(bank4[:, 0:SEQ_LEN], w_q[:, :], xt, start=True, stop=True)
                nc.tensor.matmul(bank4[:, SEQ_LEN:2 * SEQ_LEN], w_kv[:, 0:D], xt, start=True, stop=True)
                nc.tensor.matmul(bank5[:, 0:2 * D], xt[:, 0:TILE], w_kv[:, :], start=True, stop=True)
                nc.tensor.matmul(bank5[:, 2 * D:3 * D], xt[:, TILE:SEQ_LEN], w_kv[:, D:2 * D], start=True, stop=True)\
                  .then_inc(att["qkv_ps"], 1)

            def make_state(b):
                u = b.slot(2)
                wait_step(pe, att["kv_ready"], b)
                nc.tensor.matmul(bank5[:, 3 * D:4 * D], k_first[:, u, :], v_diagonal(u, 0), start=True, stop=True)\
                  .then_inc(att["state_ps"], 1)

            def score(b, c):
                u = b.slot(2)
                wait_step(pe, att["k_ready"], b)
                wait_step(pe, WEIGHTS_READY[c], b.after(-1))
                for g in range(2):
                    last = nc.tensor.matmul(ps_scores[c][:, g * 512:(g + 1) * 512],
                                            k_t[:, u, c * TILE:(c + 1) * TILE],
                                            q_blocks[:, u, g * 4:(g + 1) * 4, c * TILE:(c + 1) * TILE],
                                            start=True, stop=True)
                last.then_inc(SCORES_PS[c], 1)

            def mix_values(b):
                u = b.slot(2)
                wait_step(pe, att["x_ready"], b.after(-1))
                for c in range(PAIR):
                    wait_step(pe, WEIGHTS_READY[c], b)
                    if c:
                        wait_step(pe, att["state_ready"], b)
                        wait_step(pe, att["q_later_ready"], b)
                        nc.tensor.matmul(bank7[:, TILE:SEQ_LEN], state[:, u, :], q_later[:, u, :],
                                         start=True, stop=False)
                    for h in range(HEADS):
                        last = nc.tensor.matmul(bank7[:, c * TILE:(c + 1) * TILE],
                                                v_blocks[:, u, c, h * TILE:(h + 1) * TILE],
                                                weights[:, c, h * TILE:(h + 1) * TILE],
                                                start=c == 0 and h == 0, stop=h == HEADS - 1)
                last.then_inc(att["o_ps"], 1)

            def project_out(b):
                wait_step(pe, att["o_ready"], b)
                for c in range(PAIR):
                    last = nc.tensor.matmul(bank7[:, SEQ_LEN + c * D:SEQ_LEN + (c + 1) * D],
                                            o_t[:, c * TILE:(c + 1) * TILE], w_o[:, :], start=True, stop=True)
                last.then_inc(att["proj_ps"], 1)

            def middle(s):
                if s.after(1).within(PAIRS):
                    wait_step(pe, prep[1]["logits_ready"], s.after(-3))
                    transpose_norm(att, s.after(1), 0, bank6[:, 0:SEQ_LEN])
                    project(s.after(1))
                if s.within(PAIRS):
                    mix_values(s)
                if s.after(1).within(PAIRS):
                    make_state(s.after(1))
                if s.after(-2).within(PAIRS):
                    wait_step(pe, prep[1]["logits_ready"], s.after(-3))
                    transpose_norm(prep[1], s.after(-2), 1, bank6[:, SEQ_LEN:2 * SEQ_LEN])
                if s.after(1).within(PAIRS):
                    score(s.after(1), 0)
                if s.within(PAIRS):
                    project_out(s)
                if s.after(-2).within(PAIRS):
                    router(prep[1], s.after(-2), bank6[:, SEQ_LEN:2 * SEQ_LEN])
                if s.after(1).within(PAIRS):
                    score(s.after(1), 1)

            pe.wait_ge(consts_ready, 1)
            pe.wait_ge(router_loaded, 32)
            run_steps(pe, PAIRS, 2, 0, 1, first_prep)
            route_rows(0)
            pe.wait_ge(w1_low_ready, 1)
            pe.wait_ge(weights_loaded, 16 * 8)
            run_experts(0)
            pe.wait_ge(v_zeroed, 1)
            run_steps(pe, PAIRS, 2, 2, 1, middle)
            route_rows(1)
            run_experts(1)


def shape_constants():
    import numpy as np

    i = np.arange(TILE, dtype=np.float64)
    head = np.arange(D) // HEAD_DIM
    gamma = 1.0 - np.exp2(-5.0 - np.arange(HEADS, dtype=np.float64))
    scale = float(HEAD_DIM) ** -0.5
    parts = {
        "identity": np.eye(TILE),
        "same_head": head[:, None] == head[None, :],
        "query_decay": scale * gamma[head][:, None] ** (i[None, :] + 1),
        "key_decay": gamma[head][None, :] ** (TILE - 1 - i[:, None]),
        "before": i[:, None] < i[None, :],
        "column": np.broadcast_to(i[None, :], (TILE, TILE)),
        "tile_base": np.broadcast_to((np.arange(PICKS) * TILE)[None, :], (TILE, PICKS)),
        "head_rows": head[:, None] == np.arange(HEADS)[None, :],
        "low_first": np.broadcast_to((EXPERTS - np.arange(EXPERTS))[None, :], (TILE, EXPERTS)),
        "partition": i[:, None] + 1,
    }
    table = np.zeros((TILE, CONST_WIDTH), np.float32)
    for name, (a, b) in CONST_COLUMNS.items():
        table[:, a:b] = parts[name]
    distance = i[None, None, :] - i[:, None, None]
    decay = np.where(distance >= 0, scale * gamma[None, :, None] ** np.maximum(distance, 0), 0.0)
    return table, decay.reshape(TILE, HEADS * TILE).astype(np.float32)


def kernel(L0_attn_hidden_states, L0_attn_rel_pos, L0_attn_Wq, L0_attn_Wk, L0_attn_Wv, L0_attn_Wo,
           L0_ffn_router_w, L0_ffn_router_b, L0_ffn_W1, L0_ffn_b1, L0_ffn_W2, L0_ffn_b2):
    import numpy as np
    import concourse.bacc as bacc
    from concourse.bass_utils import run_bass_kernel_spmd

    table, decay = shape_constants()
    arrays = {
        "hidden_states": L0_attn_hidden_states, "router_w": L0_ffn_router_w, "router_b": L0_ffn_router_b,
        "W1": L0_ffn_W1, "b1": L0_ffn_b1, "W2": L0_ffn_W2, "b2": L0_ffn_b2,
        "Wq": L0_attn_Wq, "Wk": L0_attn_Wk, "Wv": L0_attn_Wv, "Wo": L0_attn_Wo,
        "consts": table, "score_decay": decay,
    }
    arrays = {f"in_{n}": np.ascontiguousarray(a) for n, a in arrays.items()}
    nc = bacc.Bacc("TRN2", target_bir_lowering=False, num_devices=1)
    ins = [nc.dram_tensor(n, a.shape, mybir.dt.from_np(a.dtype), kind="ExternalInput").ap()
           for n, a in arrays.items()]
    out = nc.dram_tensor("out_rows", (SEQS, SEQ_LEN, D), FP32, kind="ExternalOutput").ap()
    build(nc, *ins, out)
    return run_bass_kernel_spmd(nc, [arrays], core_ids=[0]).results[0]["out_rows"]
```

```python
from contextlib import ExitStack

import concourse.bass as bass
from concourse import mybir

FP32 = mybir.dt.float32
FP32R = mybir.dt.float32r
BF16 = mybir.dt.bfloat16
I32 = mybir.dt.int32
U32 = mybir.dt.uint32
ALU = mybir.AluOpType
ACT = mybir.ActivationFunctionType
AXX = mybir.AxisListType.X

SEQS, SEQ_LEN, D = 16, 256, 128
EXPERTS, FF = 8, 512
HEADS = 8
HEAD_DIM = D // HEADS
EPS = 1e-5
TILE = 128
ROWS = SEQS * SEQ_LEN
ROW_TILES = ROWS // TILE
PAIR = SEQ_LEN // TILE
PAIRS = ROW_TILES // PAIR
TOP_K = 2
PICKS = TOP_K * ROW_TILES
FF_CHUNKS = FF // TILE
SLOT_TILES = PICKS + EXPERTS - 1
EXPERT_STEP = FF + FF_CHUNKS
WEIGHT_LOADS = 2 * EXPERTS + 7
HOT = 8
FAR_BELOW = -3.0e38
AHEAD = 7
NOWHERE = float(1 << 20)

CONST_COLUMNS = {}
_at = 0
for _name, _width in (("identity", TILE), ("same_head", D), ("query_decay", TILE), ("key_decay", D),
                      ("before", TILE), ("column", TILE),
                      ("head_rows", HEADS), ("low_first", EXPERTS), ("pick_base", 1)):
    CONST_COLUMNS[_name] = (_at, _at + _width)
    _at += _width
CONST_WIDTH = _at


class Step:

    def __init__(self, c, turn=None, unroll=1):
        self.c, self.turn, self.unroll = c, turn, unroll

    @property
    def n(self):
        return self.c if self.turn is None else self.turn * self.unroll + self.c

    def after(self, k):
        return Step(self.c + k, self.turn, self.unroll)

    def within(self, count):
        return self.turn is not None or 0 <= self.c < count

    def slot(self, ring):
        return self.c % ring

    def round(self, ring):
        return self.c // ring if self.turn is None else self.turn * (self.unroll // ring) + self.c // ring


def wait_step(eng, sem, step, per=1):
    if step.turn is None and step.c < 0:
        return
    eng.wait_ge(sem, (step.n + 1) * per)


def wait_slot(eng, sems, step, per=16):
    if step.turn is None and step.c < 0:
        return
    ring = len(sems)
    eng.wait_ge(sems[step.slot(ring)], (step.round(ring) + 1) * per)


def run_steps(eng, count, unroll, lag, lead, body, group=None, tail=0):
    first = unroll + lag
    turns = max(0, (count - lead - tail - first) // unroll)
    for c in range(-lead, first):
        body(Step(c))
    if turns:
        with eng.Fori(0, turns) as turn:
            if group is not None:
                group(Step(first, turn, unroll))
            for c in range(first, first + unroll):
                body(Step(c, turn, unroll))
    for c in range(first + turns * unroll, count + lag):
        body(Step(c))


def build(nc, x_in, router_w, router_b, W1, b1, W2, b2, Wq, Wk, Wv, Wo, consts_in, score_decay_in, out):
    ctx = ExitStack()
    with ctx:
        def sb(name, shape, dt=FP32):
            return ctx.enter_context(nc.sbuf_tensor(name, shape, dt))

        def psum(name, width):
            return ctx.enter_context(nc.psum_tensor(name, [TILE, width], FP32))

        def sem(name):
            return ctx.enter_context(nc.semaphore(name))

        def sems(names, suffix):
            return {n: sem(f"{n}_{suffix}") for n in names.split()}

        def ring(name, count):
            return [sem(f"{name}_{i}") for i in range(count)]

        norm_rows = nc.dram_tensor("norm_rows", (ROWS, D), FP32, kind="Internal").ap()
        pick_rows = nc.dram_tensor("pick_rows", (TOP_K * ROWS, D), FP32, kind="Internal").ap()
        slot_rows = nc.dram_tensor("slot_rows", (SLOT_TILES * TILE, D), FP32, kind="Internal").ap()

        x = sb("x_rows", [TILE, ROW_TILES * D])
        consts = sb("consts", [TILE, CONST_WIDTH])
        const = {n: consts[:, a:b] for n, (a, b) in CONST_COLUMNS.items()}
        score_decay = sb("score_decay", [TILE, HEADS * TILE])
        w_q = sb("w_q", [D, D])
        w_kv = sb("w_kv", [D, 2 * D])
        w_o = sb("w_o", [D, D])
        w_router = sb("w_router", [D, TILE])
        bias_router = sb("bias_router", [TILE, EXPERTS])
        w1 = sb("w1", [D, EXPERTS * EXPERT_STEP])
        w2 = sb("w2", [TILE, EXPERTS * EXPERT_STEP])
        bias2 = sb("bias2", [TILE, EXPERTS * EXPERT_STEP])
        bias1_rows = sb("bias1_rows", [EXPERTS * FF_CHUNKS, TILE])
        before_bf = sb("before_bf", [TILE, TILE], BF16)
        ones_bf = sb("ones_bf", [TILE, TILE], BF16)
        ones_row = sb("ones_row", [TILE, EXPERTS * ROW_TILES])
        column_bf = sb("column_bf", [TILE, TILE], BF16)

        wait_carrier = sb("wait_carrier", [TILE, 1])
        stats = sb("stats", [TILE, 2, 2, PAIR, 6])
        moments = sb("moments", [TILE, 2, 2, PAIR, 2])
        var_eps = sb("var_eps", [TILE, 2, 2, PAIR])
        inv_var = sb("inv_var", [TILE, 2, 2, PAIR])
        inv_dev = sb("inv_dev", [TILE, 2, 2, PAIR])
        offset_dev = sb("offset_dev", [TILE, 2, 2, PAIR])
        norm = sb("norm", [TILE, 2, 2, PAIR * D])
        norm_first = sb("norm_first", [TILE, 4, PAIR * D])
        norm_t = sb("norm_t", [D, 2, 2, PAIR * TILE])
        logits = sb("logits", [TILE, ROW_TILES, EXPERTS])

        def per_expert(name, dt=FP32):
            return sb(name, [TILE, ROW_TILES, EXPERTS], dt)
        best = sb("best", [TILE, TOP_K, ROW_TILES])
        is_best = per_expert("is_best")
        ranked = per_expert("ranked")
        first_rank = sb("first_rank", [TILE, ROW_TILES])
        picks = sb("picks", [TILE, TOP_K, ROW_TILES, EXPERTS])
        pick = [picks[:, k, :, :] for k in range(TOP_K)]
        placed = sb("placed", [TILE, TOP_K, ROW_TILES, EXPERTS])
        other_logits = per_expert("other_logits")
        picked_bf = per_expert("picked_bf", BF16)
        counts = sb("counts", [TILE, EXPERTS, ROW_TILES])
        running = sb("running", [TILE, EXPERTS * ROW_TILES])
        total = sb("total", [TILE, EXPERTS + 1])
        padded_f = sb("padded_f", [TILE, EXPERTS])
        padded_i = sb("padded_i", [TILE, EXPERTS], I32)
        ends = sb("ends", [TILE, EXPERTS + 1])
        shift = sb("shift", [TILE, EXPERTS])
        place = per_expert("place")
        place_f = sb("place_f", [TILE, ROW_TILES, TOP_K])
        place_i = sb("place_i", [TILE, PICKS], I32)
        place_part_i = sb("place_part_i", [TILE, 2, PICKS], I32)
        place_low = sb("place_low", [TILE, PICKS])
        gap = sb("gap", [TILE, ROW_TILES])
        gap_exp = sb("gap_exp", [TILE, ROW_TILES])
        gap_sum = sb("gap_sum", [TILE, ROW_TILES])
        gate = sb("gate", [TILE, TOP_K, ROW_TILES])
        place_high_bf = sb("place_high_bf", [TILE, PICKS], BF16)
        V_STEP = TILE + HEAD_DIM
        v_or_hot = sb("v_or_hot", [TILE, 2 * PAIR * HEADS * V_STEP])
        hot_bf = v_or_hot[:, :].bitcast(BF16)
        low_hot = hot_bf[:, 0:2 * HOT * TILE].rearrange("p (u i n) -> p u i n", u=2, i=HOT)
        hot_bf = hot_bf[:, 2 * HOT * TILE:]
        high_hot = hot_bf[:, 0:2 * HOT * SLOT_TILES].rearrange("p (u i n) -> p u i n", u=2, i=HOT)
        hot_bf = hot_bf[:, 2 * HOT * SLOT_TILES:]
        high_value = hot_bf[:, 0:2 * HOT * 2 * SLOT_TILES].rearrange("p (u i v n) -> p u i v n", u=2, i=HOT, v=2)
        slot_row_f = sb("slot_row_f", [TILE, SLOT_TILES])
        slot_row_sum = sb("slot_row_sum", [TILE, SLOT_TILES])
        slot_row_i = sb("slot_row_i", [TILE, SLOT_TILES], I32)
        spare = sb("spare", [TILE, SLOT_TILES])
        slot_table = sb("slot_table", [TILE, SLOT_TILES + AHEAD, 2], U32)
        past_end = sb("past_end", [TILE, SLOT_TILES, EXPERTS - 1])
        tile_start = sb("tile_start", [TILE, SLOT_TILES])
        tile_expert_f = sb("tile_expert_f", [TILE, SLOT_TILES])
        expert_offset = sb("expert_offset", [TILE, SLOT_TILES], I32)

        row_index = sb("row_index", [TILE, 4 * 2], U32)
        got = sb("got", [TILE, 4, D])
        got_t = sb("got_t", [D, 2, TILE])
        w1_now = sb("w1_now", [D, 2, EXPERT_STEP])
        hidden_t = sb("hidden_t", [TILE, 2, FF])
        result = sb("result", [TILE, 4, D])

        back_index = sb("back_index", [TILE, 4 * PAIR * TOP_K], U32)
        back = sb("back", [TILE, 4, PAIR, TOP_K, D])

        def last_back(b, count):
            width = PAIR * TOP_K * D
            half = (w1, w2)[b // (PAIRS // 2)]
            b %= PAIRS // 2
            return half[:, b * width:(b + count) * width]

        q_high = sb("q_high", [D, 2, HEADS, SEQ_LEN], FP32R)
        q_low = sb("q_low", [D, 2, HEADS, SEQ_LEN], FP32R)
        q_t_high = sb("q_t_high", [D, SEQ_LEN], FP32R)
        q_t_low = sb("q_t_low", [D, 2, SEQ_LEN])
        k_high = sb("k_high", [D, 2, SEQ_LEN], FP32R)
        k_low = sb("k_low", [D, 2, SEQ_LEN], FP32R)
        q_later = sb("q_later", [D, 2, TILE])
        k_first = sb("k_first", [TILE, 2, D])
        v_blocks = v_or_hot[:, :].rearrange("p (u c s) -> p u c s", u=2, c=PAIR)
        state = sb("state", [D, 2, D])
        weights = sb("weights", [TILE, PAIR, HEADS * TILE])
        o_t = sb("o_t", [D, SEQ_LEN])

        def v_diagonal(u, c):
            return v_blocks[:, u, c, :].rearrange("p (h s) -> p h s", s=V_STEP)[:, :, 0:HEAD_DIM]

        bank01, bank23 = psum("bank01", 1024), psum("bank23", 1024)
        bank4, bank5, bank6, bank7 = (psum(f"bank{i}", 512) for i in range(4, 8))
        ps_scores = [bank01, bank23]
        ps_got_t = [bank01[:, 0:TILE], bank01[:, 512:512 + TILE]]
        ps_hidden_t = [bank4, bank5]
        ps_logits = [bank[:, 0:SEQ_LEN] for bank in (bank01, bank23, bank4, bank5)]
        ps_result = [bank6[:, 0:D], bank7[:, 0:D]]

        bias_router_loaded = sem("bias_router_loaded")
        consts_loaded, router_loaded, weights_loaded = sem("consts_loaded"), sem("router_loaded"), sem("weights_loaded")
        x_loaded = {piece: sem(f"x_loaded_{piece.start}") for piece in (range(0, 2), range(2, 5), range(5, PAIRS))}
        consts_ready, bias1_ps, bias1_ready = sem("consts_ready"), sem("bias1_ps"), sem("bias1_ready")
        router_zeroed, table_zeroed, v_zeroed = sem("router_zeroed"), sem("table_zeroed"), sem("v_zeroed")
        prep = [sems("stats_done moments_done var_ready inv_ready dev_ready offset_ready norm_ready norm_t_ps "
                     "norm_t_ready "
                     "logits_ps logits_ready", f"prep{f}") for f in range(2)]
        rows_stored = [ring(f"rows_stored_prep{f}", (4, 2)[f]) for f in range(2)]
        route = [sems("chain picked ranks_ps gap_ready exp_ready high_ready column_ready base_ready low_ready "
                      "table_ps rows_ready experts_ready", f"route{f}") for f in range(2)]
        expert = [sems("index_copied got_t_ps got_t_ready w1_copied hidden_t_ps hidden_t_ready result_ps "
                       "result_ready", f"ffn{f}") for f in range(2)]
        gathered = [ring(f"gathered_ffn{f}", 4) for f in range(2)]
        result_stored = [ring(f"result_stored_ffn{f}", 4) for f in range(2)]
        back_gathered, back_loaded = ring("back_gathered", 4), ring("back_loaded", PAIRS // 2)
        comb = [sems("index_copied first_added added", f"back{f}") for f in range(2)]
        att = sems("stats_done moments_done var_ready inv_ready dev_ready offset_ready norm_ready norm_t_ps "
                   "norm_t_ready qk_ps kv_ps q_t_high_ready q_t_low_ready k_high_ready k_ready q_high_ready q_low_ready kv_ready q_later_ready state_ps state_ready scores_ps0 scores_ps1 weights_ready0 "
                   "weights_ready1 o_ps o_ready proj_ps x_ready", "att")
        out_stored = sem("out_stored")

        SCORES_PS = [att["scores_ps0"], att["scores_ps1"]]
        WEIGHTS_READY = [att["weights_ready0"], att["weights_ready1"]]

        def norm_slot(s, which, b):
            return norm_first[:, b.slot(4), :] if s is prep[0] else norm[:, which, b.slot(2), :]

        def x_pair(step):
            return x[:, bass.ds(step.n * (PAIR * D), PAIR * D)]

        block = ctx.enter_context(nc.Block())

        @block.sync
        def _(sp):
            def rows_of(a, b):
                return x_in[a:b, :, :].rearrange("b (t p) d -> p (b t) d", p=TILE)

            for piece, loaded in x_loaded.items():
                sp.dma_start(x[:, piece.start * PAIR * D:piece.stop * PAIR * D].rearrange("p (t d) -> p t d", d=D),
                             rows_of(piece.start, piece.stop)).then_inc(loaded, 16)
            def store_norm(f, b, which):
                wait_step(sp, prep[f]["norm_ready"], b)
                sp.dma_start(norm_rows.rearrange("(p c) d -> p (c d)", p=TILE)[:, bass.ds(b.n * (PAIR * D), PAIR * D)],
                             norm_slot(prep[f], which, b)).then_inc(rows_stored[f][b.slot((4, 2)[f])], 16)

            def store_and_load(e):
                b = Step(e.c * 2, e.turn, e.unroll * 2)
                store_norm(0, b, 1)
                sp.dma_start(w1[:, bass.ds(e.n * EXPERT_STEP, FF)], W1[bass.ds(e.n, 1), :, :].rearrange("e p f -> p (e f)"))\
                  .then_inc(weights_loaded, 16)
                store_norm(0, b.after(1), 1)
                sp.dma_start(w2[:, bass.ds(e.n * EXPERT_STEP, FF)].rearrange("p (c d) -> p c d", d=D),
                             W2[bass.ds(e.n, 1), :, :].rearrange("e (c p) d -> p (e c) d", p=TILE))\
                  .then_inc(weights_loaded, 16)

            def store_result(f, j):
                wait_step(sp, expert[f]["result_ready"], j)
                sp.dma_start(slot_rows[bass.ds(j.n * TILE, TILE), :], result[:, j.slot(4), :])\
                  .then_inc(result_stored[f][j.slot(4)], 16)

            def load_back(i):
                width = 2 * PAIR * TOP_K * D
                sp.dma_start(last_back(2 * i, 2), pick_rows.rearrange("(p c) d -> p (c d)", p=TILE)
                             [:, i * width:(i + 1) * width]).then_inc(back_loaded[i], 16)

            def store_out(i):
                sp.wait_ge(comb[1]["added"], (2 * i + 2) * PAIR)
                sp.dma_start(out[2 * i:2 * i + 2, :, :].rearrange("b (t p) d -> p (b t) d", p=TILE),
                             x[:, 2 * i * PAIR * D:(2 * i + 2) * PAIR * D].rearrange("p (t d) -> p t d", d=D))\
                  .then_inc(out_stored, 16)

            run_steps(sp, EXPERTS, 2, 0, 0, store_and_load)
            sp.dma_start(bias1_rows[:, :], b1.rearrange("e (c p) -> (e c) p", p=TILE)).then_inc(weights_loaded, 16)
            sp.dma_start(bias2[:, :].rearrange("p (e f) -> p e f", e=EXPERTS)[:, :, 0:D],
                         b2.rearrange("e d -> (e d)").partition_broadcast(TILE)
                           .rearrange("p (e d) -> p e d", e=EXPERTS)).then_inc(weights_loaded, 16)
            for w, source in ((w_q[:, :], Wq), (w_kv[:, 0:D], Wk), (w_kv[:, D:2 * D], Wv), (w_o[:, :], Wo),
                              (score_decay[:, :], score_decay_in)):
                sp.dma_start(w, source).then_inc(weights_loaded, 16)
            run_steps(sp, SLOT_TILES, 4, 0, 0, lambda j: store_result(0, j))
            run_steps(sp, PAIRS, 2, 0, 0, lambda b: store_norm(1, b, 1))
            for s in range(4):
                sp.wait_ge(result_stored[1][s], len(range(s, SLOT_TILES, 4)) * 16)
            for i in range(PAIRS // 2):
                load_back(i)
            for i in range(PAIRS // 2):
                store_out(i)
            sp.wait_ge(out_stored, PAIRS // 2 * 16)

        @block.gpsimd
        def _(pool):
            nc.gpsimd.memset(slot_table[:, :, :].rearrange("p j c -> p (j c)"), 0).then_inc(table_zeroed, 1)

            def copy_row_index(f, j):
                nc.gpsimd.tensor_copy(row_index[:, j.slot(4) * 2:j.slot(4) * 2 + 2],
                                      slot_table[:, bass.ds(j.n, 1), :].rearrange("p a c -> p (a c)"))\
                  .then_inc(expert[f]["index_copied"], 1)

            def gather_tile(f, j):
                n = j.slot(4) * 2
                nc.gpsimd.indirect_dma_start(
                    out=got[:, j.slot(4), :], out_offset=None, in_=norm_rows,
                    in_offset=bass.IndirectOffsetOnAxis(ap=row_index[:, n:n + 1], axis=0))\
                  .then_inc(gathered[f][j.slot(4)], 16)

            def gather_step(j):
                wait_step(pool, expert[0]["index_copied"], j)
                wait_step(pool, expert[0]["got_t_ps"], j.after(-4))
                if j.after(1).within(SLOT_TILES):
                    wait_slot(pool, gathered[0], j.after(1 - 4))
                    copy_row_index(0, j.after(1))
                gather_tile(0, j)

            def gather_scatter_step(j):
                done = j.after(-AHEAD)
                wait_step(pool, expert[1]["index_copied"], j)
                if j.within(SLOT_TILES):
                    wait_step(pool, expert[1]["got_t_ps"], j.after(-4))
                if done.within(SLOT_TILES):
                    wait_step(pool, expert[1]["result_ready"], done)
                if j.after(1).within(SLOT_TILES + AHEAD):
                    if j.after(1 - 4).within(SLOT_TILES):
                        wait_slot(pool, gathered[1], j.after(1 - 4))
                    wait_slot(pool, result_stored[1], done.after(1 - 4))
                    copy_row_index(1, j.after(1))
                if j.within(SLOT_TILES):
                    gather_tile(1, j)
                if done.within(SLOT_TILES):
                    n = j.slot(4) * 2 + 1
                    nc.gpsimd.indirect_dma_start(
                        out=pick_rows, out_offset=bass.IndirectOffsetOnAxis(ap=row_index[:, n:n + 1], axis=0),
                        in_=result[:, done.slot(4), :], in_offset=None, bounds_check=TOP_K * ROWS - 1,
                        oob_is_err=False).then_inc(result_stored[1][done.slot(4)], 16)

            def copy_back_index(b):
                u = b.slot(4)
                nc.gpsimd.tensor_copy(back_index[:, u * 4:u * 4 + 4],
                                      place_i[:, bass.ds(b.n * (PAIR * TOP_K), PAIR * TOP_K)].bitcast(U32))\
                  .then_inc(comb[0]["index_copied"], 1)

            def place_low_queries(b):
                u = b.slot(2)
                wait_step(pool, att["q_t_low_ready"], b)
                wait_step(pool, SCORES_PS[1], b.after(-2))
                for c in range(PAIR):
                    nc.gpsimd.tensor_tensor(q_low[:, u, :, c * TILE:(c + 1) * TILE],
                                            q_t_low[:, u, c * TILE:(c + 1) * TILE].unsqueeze(1)
                                            .to_broadcast([D, HEADS, TILE]),
                                            const["head_rows"].unsqueeze(2).to_broadcast([D, HEADS, TILE]), ALU.mult)\
                      .then_inc(att["q_low_ready"], 1)

            def gather_back(b):
                u = b.slot(4)
                wait_step(pool, comb[0]["index_copied"], b)
                wait_step(pool, comb[0]["added"], b.after(-4), PAIR)
                if b.after(1).within(PAIRS):
                    wait_slot(pool, back_gathered, b.after(1 - 4), 16 * 4)
                    copy_back_index(b.after(1))
                for t in range(PAIR):
                    for k in range(TOP_K):
                        n = u * 4 + t * TOP_K + k
                        nc.gpsimd.indirect_dma_start(
                            out=back[:, u, t, k, :], out_offset=None, in_=slot_rows,
                            in_offset=bass.IndirectOffsetOnAxis(ap=back_index[:, n:n + 1], axis=0))\
                          .then_inc(back_gathered[u], 16)

            def table_and_rows(f):
                pool.wait_ge(route[f]["rows_ready"], 1)
                for stored in rows_stored[f]:
                    pool.wait_ge(stored, PAIRS // len(rows_stored[f]) * 16)

            def column_numbers(f):
                def group(g):
                    u = g.slot(2)
                    wait_step(pool, route[f]["high_ready"], g)
                    wait_step(pool, route[f]["table_ps"], g.after(-2))
                    nc.gpsimd.tensor_tensor(high_value[:, u, :, 0, :], high_hot[:, u, :, :],
                                            column_bf[:, bass.ds(g.n * HOT, HOT)].unsqueeze(2)
                                            .to_broadcast([TILE, HOT, SLOT_TILES]), ALU.mult)\
                      .then_inc(route[f]["column_ready"], 1)
                run_steps(pool, PICKS // HOT, 2, 0, 0, group)

            column_numbers(0)
            table_and_rows(0)
            copy_row_index(0, Step(0))
            run_steps(pool, SLOT_TILES, 4, 0, 0, gather_step, tail=1)
            nc.gpsimd.memset(v_or_hot[:, :], 0.0).then_inc(v_zeroed, 1)
            for s in range(4):
                pool.wait_ge(result_stored[0][s], len(range(s, SLOT_TILES, 4)) * 16)
            copy_back_index(Step(0))

            def middle(s):
                if s.after(1).within(PAIRS):
                    place_low_queries(s.after(1))
                if s.after(5).within(PAIRS):
                    gather_back(s.after(5))

            run_steps(pool, PAIRS, 4, 0, 5, middle, tail=1)
            column_numbers(1)
            table_and_rows(1)
            copy_row_index(1, Step(0))
            run_steps(pool, SLOT_TILES, 4, 8, 0, lambda j: gather_scatter_step(j)
                      if j.within(SLOT_TILES + AHEAD) else None)

        @block.scalar
        def _(act):
            act.dma_start(consts[:, :], consts_in).then_inc(consts_loaded, 16)
            act.dma_start(w_router[:, 0:EXPERTS], router_w).then_inc(router_loaded, 16)
            act.dma_start(bias_router[:, :], router_b.partition_broadcast(TILE))\
              .then_inc(bias_router_loaded, 16)

            def invert_deviation(s, b, which):
                u = b.slot(2)
                wait_step(act, s["inv_ready"], b)
                nc.scalar.activation(inv_dev[:, which, u, :], inv_var[:, which, u, :], ACT.Sqrt)\
                  .then_inc(s["dev_ready"], 1)

            def normalise(s, b, which, reader, stored=None):
                u = b.slot(2)
                wait_step(act, s["offset_ready"], b)
                last = b.after(-4 if s is prep[0] else -2)
                wait_step(act, reader, last)
                if stored is not None:
                    wait_slot(act, stored, last)
                for t in range(PAIR):
                    last = nc.scalar.activation(norm_slot(s, which, b)[:, t * D:(t + 1) * D],
                                                x[:, bass.ds((b.n * PAIR + t) * D, D)], ACT.Identity,
                                                bias=offset_dev[:, which, u, t:t + 1],
                                                scale=inv_dev[:, which, u, t:t + 1])
                last.then_inc(s["norm_ready"], 1)

            def copy_norm_t(s, b, which, ps, readers):
                wait_step(act, s["norm_t_ps"], b)
                wait_step(act, readers, b.after(-2))
                nc.scalar.activation(norm_t[:, which, b.slot(2), :], ps, ACT.Copy)\
                  .then_inc(s["norm_t_ready"], 1)

            def first_prep(b):
                if b.after(1).within(PAIRS):
                    normalise(prep[0], b.after(1), 1, prep[0]["norm_t_ps"], rows_stored[0])
                if b.after(2).within(PAIRS):
                    invert_deviation(prep[0], b.after(2), 1)
                if b.within(PAIRS):
                    copy_norm_t(prep[0], b, 1, (bank6, bank7)[b.slot(2)][:, 0:SEQ_LEN], prep[0]["logits_ps"])

            def exp_gap(f):
                act.wait_ge(route[f]["gap_ready"], 1)
                nc.scalar.activation(gap_exp[:, :], gap[:, :], ACT.Exp).then_inc(route[f]["exp_ready"], 1)

            def pick_bases(f):
                def group(g):
                    u = g.slot(2)
                    wait_step(act, route[f]["high_ready"], g)
                    wait_step(act, route[f]["table_ps"], g.after(-2))
                    nc.scalar.activation(high_value[:, u, :, 1, :], high_hot[:, u, :, :], ACT.Copy,
                                         scale=const["pick_base"]).then_inc(route[f]["base_ready"], 1)
                run_steps(act, PICKS // HOT, 2, 0, 0, group)

            def copy_got_t(f, j):
                wait_step(act, expert[f]["got_t_ps"], j)
                wait_step(act, expert[f]["hidden_t_ps"], j.after(-2))
                nc.scalar.activation(got_t[:, j.slot(2), :], ps_got_t[j.slot(2)], ACT.Copy)\
                  .then_inc(expert[f]["got_t_ready"], 1)

            def relu_tile(f, j):
                u = j.slot(2)
                wait_step(act, expert[f]["hidden_t_ps"], j)
                wait_step(act, expert[f]["result_ps"], j.after(-2))
                for c in range(FF_CHUNKS):
                    last = nc.scalar.activation(hidden_t[:, u, c * TILE:(c + 1) * TILE],
                                                ps_hidden_t[u][:, c * TILE:(c + 1) * TILE], ACT.Relu,
                                                bias=w1_now[:, u, FF + c:FF + c + 1])
                last.then_inc(expert[f]["hidden_t_ready"], 1)

            def expert_step(f, s):
                if s.after(1).within(SLOT_TILES):
                    relu_tile(f, s.after(1))
                if s.after(3).within(SLOT_TILES):
                    copy_got_t(f, s.after(3))

            def place_high_queries(b):
                u = b.slot(2)
                wait_step(act, att["q_t_high_ready"], b)
                wait_step(act, SCORES_PS[1], b.after(-2))
                for g in range(2):
                    for h in range(g * HEADS // 2, (g + 1) * HEADS // 2):
                        last = nc.scalar.activation(q_high[:, u, h, :], q_t_high[:, :].bitcast(FP32), ACT.Copy,
                                                    scale=const["head_rows"][:, h:h + 1])
                    last.then_inc(att["q_high_ready"], 1)

            def copy_o(b):
                wait_step(act, att["o_ps"], b)
                wait_step(act, att["proj_ps"], b.after(-1))
                nc.scalar.activation(o_t[:, :], bank7[:, 0:SEQ_LEN], ACT.Copy).then_inc(att["o_ready"], 1)

            def middle(s):
                if s.after(-1).within(PAIRS):
                    invert_deviation(prep[1], s.after(-1), 1)
                    normalise(prep[1], s.after(-1), 1, prep[1]["norm_t_ps"], rows_stored[1])
                if s.after(1).within(PAIRS):
                    place_high_queries(s.after(1))
                if s.within(PAIRS):
                    copy_o(s)
                if s.after(2).within(PAIRS):
                    invert_deviation(att, s.after(2), 0)
                    normalise(att, s.after(2), 0, att["norm_t_ps"])
                if s.after(2).within(PAIRS):
                    copy_norm_t(att, s.after(2), 0, bank6[:, 0:SEQ_LEN], att["kv_ps"])
                if s.after(-1).within(PAIRS):
                    copy_norm_t(prep[1], s.after(-1), 1, bank6[:, SEQ_LEN:2 * SEQ_LEN], prep[1]["logits_ps"])

            run_steps(act, PAIRS, 4, 0, 2, first_prep)
            exp_gap(0)
            pick_bases(0)
            run_steps(act, SLOT_TILES, 4, 0, 3, lambda s: expert_step(0, s))
            run_steps(act, PAIRS, 2, 2, 2, middle)
            exp_gap(1)
            pick_bases(1)
            run_steps(act, SLOT_TILES, 4, 0, 3, lambda s: expert_step(1, s))

        @block.vector
        def _(dve):
            nc.vector.memset(w_router[:, EXPERTS:], 0.0).then_inc(router_zeroed, 1)
            nc.vector.memset(ones_bf[:, :], 1.0)
            nc.vector.memset(ones_row[:, :], 1.0)
            nc.vector.memset(total[:, 0:1], 0.0)
            nc.vector.memset(ends[:, 0:1], 0.0)

            def convert_constants():
                dve.wait_ge(consts_loaded, 16)
                nc.vector.tensor_copy(before_bf[:, :], const["before"])
                nc.vector.tensor_copy(column_bf[:, :], const["column"])
                nc.vector.tensor_scalar(tile_start[:, :], const["column"][:, 0:SLOT_TILES], float(TILE), None,
                                        ALU.mult).then_inc(consts_ready, 1)

            def carry_wait():
                nc.vector.memset(wait_carrier[:, :], 0.0)

            def take_stats(s, b, which):
                carry_wait()
                for t in range(PAIR):
                    last = nc.vector.bn_stats(stats[:, which, b.slot(2), t, :],
                                              x[:, bass.ds((b.n * PAIR + t) * D, D)])
                last.then_inc(s["stats_done"], 1)

            def take_moments(s, b, which):
                u = b.slot(2)
                wait_step(dve, s["stats_done"], b)
                carry_wait()
                for t in range(PAIR):
                    last = nc.vector.bn_aggr(moments[:, which, u, t, :], stats[:, which, u, t, :])
                last.then_inc(s["moments_done"], 1)

            def invert_variance(s, b, which):
                u = b.slot(2)
                wait_step(dve, s["moments_done"], b)
                nc.vector.tensor_scalar(var_eps[:, which, u, :], moments[:, which, u, :, 1], EPS, None, ALU.add)\
                  .then_inc(s["var_ready"], 1)
                wait_step(dve, s["var_ready"], b)
                nc.vector.reciprocal(inv_var[:, which, u, :], var_eps[:, which, u, :]).then_inc(s["inv_ready"], 1)

            def scale_mean(s, b, which):
                u = b.slot(2)
                wait_step(dve, s["dev_ready"], b)
                wait_step(dve, s["norm_ready"], b.after(-2))
                nc.vector.scalar_tensor_tensor(offset_dev[:, which, u, :], moments[:, which, u, :, 0], -1.0,
                                               inv_dev[:, which, u, :], ALU.mult, ALU.mult)\
                  .then_inc(s["offset_ready"], 1)

            def add_router_bias(s, b, ps):
                wait_step(dve, s["logits_ps"], b)
                nc.vector.tensor_tensor(
                    logits[:, bass.ds(b.n * PAIR, PAIR), :],
                    ps.rearrange("p (t c) -> p t c", t=PAIR)[:, :, 0:EXPERTS],
                    bias_router[:, :].unsqueeze(1).to_broadcast([TILE, PAIR, EXPERTS]), ALU.add)\
                  .then_inc(s["logits_ready"], 1)

            def first_prep(b):
                for piece, loaded in x_loaded.items():
                    if b.turn is None and b.c + 2 == piece.start:
                        dve.wait_ge(loaded, 16)
                if b.after(2).within(PAIRS):
                    take_stats(prep[0], b.after(2), 1)
                if b.after(1).within(PAIRS):
                    scale_mean(prep[0], b.after(1), 1)
                if b.after(2).within(PAIRS):
                    take_moments(prep[0], b.after(2), 1)
                if b.turn is None and b.c == 2:
                    dve.wait_ge(bias_router_loaded, 16)
                if b.after(-2).within(PAIRS):
                    add_router_bias(prep[0], b.after(-2), ps_logits[b.after(-2).slot(4)])
                if b.after(2).within(PAIRS):
                    invert_variance(prep[0], b.after(2), 1)
                if b.turn is None and b.c == 0:
                    convert_constants()

            def route_rows(f):
                r = route[f]
                done = [0]

                def link(ins):
                    done[0] += 1
                    ins.then_inc(r["chain"], 1)
                    dve.wait_ge(r["chain"], done[0])

                def over_experts(a):
                    return a.unsqueeze(2).to_broadcast([TILE, ROW_TILES, EXPERTS])

                rank = const["low_first"].unsqueeze(1).to_broadcast([TILE, ROW_TILES, EXPERTS])
                scores = logits
                for k in range(TOP_K):
                    link(nc.vector.tensor_reduce(best[:, k, :], scores[:, :, :], AXX, ALU.max))
                    link(nc.vector.tensor_tensor(is_best[:, :, :], scores[:, :, :], over_experts(best[:, k, :]),
                                                 ALU.is_equal))
                    link(nc.vector.tensor_tensor(ranked[:, :, :], is_best[:, :, :], rank, ALU.mult))
                    link(nc.vector.tensor_reduce(first_rank[:, :], ranked[:, :, :], AXX, ALU.max))
                    link(nc.vector.tensor_tensor(pick[k][:, :, :], over_experts(first_rank[:, :]), rank,
                                                 ALU.is_equal))
                    if k == 0:
                        link(nc.vector.scalar_tensor_tensor(other_logits[:, :, :], pick[0][:, :, :], FAR_BELOW,
                                                            logits[:, :, :], ALU.mult, ALU.add))
                        scores = other_logits
                nc.vector.tensor_tensor(picked_bf[:, :, :], pick[0][:, :, :], pick[1][:, :, :], ALU.add)\
                  .then_inc(r["picked"], 1)
                nc.vector.tensor_tensor(gap[:, :], best[:, 1, :], best[:, 0, :], ALU.subtract)\
                  .then_inc(r["gap_ready"], 1)
                dve.wait_ge(r["ranks_ps"], 1)
                link(nc.vector.tensor_copy(counts[:, :, :],
                                           bank4[:, 256:512].rearrange("p (t e) -> p e t", e=EXPERTS)))
                link(nc.vector.tensor_tensor_scan(running[:, :], ones_row[:, :],
                                                  counts[:, :, :].rearrange("p e t -> p (e t)"), 0.0,
                                                  ALU.mult, ALU.add))
                running_e = running[:, :].rearrange("p (e t) -> p e t", e=EXPERTS)
                nc.vector.tensor_copy(total[:, 1:EXPERTS + 1], running_e[:, :, ROW_TILES - 1])
                link(nc.vector.tensor_tensor(counts[:, :, :], running_e, counts[:, :, :], ALU.subtract))
                link(nc.vector.scalar_tensor_tensor(padded_i[:, :], total[:, 1:EXPERTS + 1], float(TILE - 1),
                                                    total[:, 0:EXPERTS], ALU.add, ALU.subtract))
                link(nc.vector.tensor_scalar(padded_i[:, :], padded_i[:, :], -TILE, None, ALU.bitwise_and))
                link(nc.vector.tensor_copy(padded_f[:, :], padded_i[:, :]))
                link(nc.vector.tensor_tensor_scan(ends[:, 1:EXPERTS + 1], ones_row[:, 0:EXPERTS], padded_f[:, :],
                                                  0.0, ALU.mult, ALU.add))
                link(nc.vector.tensor_tensor(shift[:, :], ends[:, 0:EXPERTS], total[:, 0:EXPERTS], ALU.subtract))
                link(nc.vector.tensor_tensor(counts[:, :, :], counts[:, :, :],
                                             shift[:, :].unsqueeze(2).to_broadcast([TILE, EXPERTS, ROW_TILES]),
                                             ALU.add))
                link(nc.vector.tensor_tensor(place[:, :, :],
                                             bank4[:, 0:256].rearrange("p (t e) -> p t e", e=EXPERTS),
                                             counts[:, :, :].rearrange("p e t -> p t e"), ALU.add))
                link(nc.vector.tensor_tensor(placed[:, :, :, :].rearrange("p k t e -> p k (t e)"),
                                             picks[:, :, :, :].rearrange("p k t e -> p k (t e)"),
                                             place[:, :, :].rearrange("p t e -> p (t e)").unsqueeze(1)
                                             .to_broadcast([TILE, TOP_K, ROW_TILES * EXPERTS]), ALU.mult))
                link(nc.vector.tensor_reduce(place_f[:, :, :].rearrange("p t k -> p k t"), placed[:, :, :, :], AXX,
                                             ALU.add))
                link(nc.vector.tensor_copy(place_i[:, :], place_f[:, :, :].rearrange("p t k -> p (t k)")))
                nc.vector.tensor_scalar(place_part_i[:, 0, :], place_i[:, :], TILE - 1, None, ALU.bitwise_and)
                link(nc.vector.tensor_scalar(place_part_i[:, 1, :], place_i[:, :], TILE.bit_length() - 1, None,
                                             ALU.logical_shift_right))
                nc.vector.tensor_copy(place_low[:, :], place_part_i[:, 0, :])
                link(nc.vector.tensor_copy(place_high_bf[:, :], place_part_i[:, 1, :]))

                def hot_group(g):
                    u = g.slot(2)
                    wait_step(dve, r["table_ps"], g.after(-2))
                    nc.vector.tensor_tensor(high_hot[:, u, :, :],
                                            column_bf[:, 0:SLOT_TILES].unsqueeze(1).to_broadcast([TILE, HOT, SLOT_TILES]),
                                            place_high_bf[:, bass.ds(g.n * HOT, HOT)].unsqueeze(2)
                                            .to_broadcast([TILE, HOT, SLOT_TILES]), ALU.is_equal)\
                      .then_inc(r["high_ready"], 1)
                    for i in range(HOT):
                        last = nc.vector.tensor_scalar(low_hot[:, u, i, :], column_bf[:, :],
                                                       place_low[:, bass.ds(g.n * HOT + i, 1)], None, ALU.is_equal)
                    last.then_inc(r["low_ready"], 1)

                run_steps(dve, PICKS // HOT, 2, 0, 0, hot_group)
                dve.wait_ge(table_zeroed, 1)
                dve.wait_ge(r["table_ps"], PICKS // HOT)
                link(nc.vector.tensor_copy(slot_row_f[:, :], bank5[:, 0:SLOT_TILES]))
                link(nc.vector.tensor_tensor(slot_row_sum[:, :], slot_row_f[:, :],
                                             bank5[:, SLOT_TILES:2 * SLOT_TILES], ALU.add))
                link(nc.vector.tensor_scalar(slot_row_i[:, :], slot_row_sum[:, :], -float(PICKS), 0.0, ALU.add,
                                             ALU.max))
                if f == 1:
                    link(nc.vector.tensor_scalar(spare[:, :], slot_row_sum[:, :], 0.0, NOWHERE, ALU.is_equal,
                                                 ALU.mult))
                    nc.vector.scalar_tensor_tensor(slot_table[:, AHEAD:, 1], slot_row_sum[:, :], -float(PICKS), spare[:, :],
                                                   ALU.add, ALU.add)
                nc.vector.tensor_scalar(slot_table[:, 0:SLOT_TILES, 0].bitcast(I32), slot_row_i[:, :],
                                        TOP_K.bit_length() - 1, None, ALU.logical_shift_right).then_inc(r["rows_ready"], 1)
                link(nc.vector.tensor_tensor(
                    past_end[:, :, :], tile_start[:, :].unsqueeze(2).to_broadcast([TILE, SLOT_TILES, EXPERTS - 1]),
                    ends[:, 1:EXPERTS].unsqueeze(1).to_broadcast([TILE, SLOT_TILES, EXPERTS - 1]), ALU.is_ge))
                link(nc.vector.tensor_reduce(tile_expert_f[:, :], past_end[:, :, :], AXX, ALU.add))
                nc.vector.tensor_scalar(expert_offset[:, :], tile_expert_f[:, :], float(EXPERT_STEP), None, ALU.mult)\
                  .then_inc(r["experts_ready"], 1)
                dve.wait_ge(r["exp_ready"], 1)
                link(nc.vector.tensor_scalar(gap_sum[:, :], gap_exp[:, :], 2.0, 2.0, ALU.mult, ALU.add))
                link(nc.vector.reciprocal(gate[:, 0, :], gap_sum[:, :]))
                link(nc.vector.tensor_tensor(gate[:, 1, :], gate[:, 0, :], gap_exp[:, :], ALU.mult))

            offsets = {}

            def load_offsets(first, count):
                _, values = nc.values_load_multi_w_load_instructions(
                    expert_offset[0:1, bass.ds(first.n, count)], engines=[mybir.EngineType.DVE], min_val=0,
                    max_val=(EXPERTS - 1) * EXPERT_STEP,
                    skip_runtime_bounds_check_because="a sum of EXPERTS - 1 comparisons times EXPERT_STEP")
                for i in range(count):
                    offsets[first.turn is None, first.c + i] = values[i]

            def offset(j):
                key = (j.turn is None, j.c)
                if key not in offsets:
                    load_offsets(j, 1)
                return offsets[key]

            def copy_w1(f, j):
                at = offset(j)
                wait_step(dve, expert[f]["hidden_t_ready"], j.after(-2))
                nc.vector.tensor_copy(w1_now[:, j.slot(2), :], w1[:, bass.ds(at, EXPERT_STEP)])\
                  .then_inc(expert[f]["w1_copied"], 1)

            def add_bias2(f, j):
                at = offset(j)
                wait_step(dve, expert[f]["result_ps"], j)
                wait_slot(dve, result_stored[f], j.after(-4))
                nc.vector.tensor_tensor(result[:, j.slot(4), :], ps_result[j.slot(2)], bias2[:, bass.ds(at, D)],
                                        ALU.add).then_inc(expert[f]["result_ready"], 1)

            def expert_step(f, s):
                if s.within(SLOT_TILES):
                    add_bias2(f, s)
                if s.after(3).within(SLOT_TILES):
                    copy_w1(f, s.after(3))

            def run_experts(f):
                offsets.clear()
                run_steps(dve, SLOT_TILES, 4, 0, 3, lambda s: expert_step(f, s),
                          group=lambda first: load_offsets(first, 7))

            def add_pick(f, k, b):
                if k:
                    wait_step(dve, comb[f]["first_added"], b, PAIR)
                elif f == 0:
                    wait_slot(dve, back_gathered, b, 16 * 4)
                elif b.c % 2 == 0:
                    dve.wait_ge(back_loaded[b.c // 2], 16)
                for t in range(PAIR):
                    row = x[:, bass.ds((b.n * PAIR + t) * D, D)]
                    if f == 0:
                        got_back = back[:, b.slot(4), t, k, :]
                    else:
                        got_back = last_back(b.c, 1)[:, (t * TOP_K + k) * D:(t * TOP_K + k + 1) * D]
                    nc.vector.scalar_tensor_tensor(row, got_back, gate[:, k, bass.ds(b.n * PAIR + t, 1)], row,
                                                   ALU.mult, ALU.add)\
                      .then_inc(comb[f]["added" if k else "first_added"], 1)

            def last_adds(s):
                if s.after(1).within(PAIRS):
                    add_pick(1, 0, s.after(1))
                if s.within(PAIRS):
                    add_pick(1, 1, s)

            def weigh_scores(b, c):
                wait_step(dve, SCORES_PS[c], b)
                wait_step(dve, att["o_ps"], b.after(-1))
                nc.vector.tensor_tensor(weights[:, c, :], ps_scores[c][:, :], score_decay[:, :], ALU.mult)\
                  .then_inc(WEIGHTS_READY[c], 1)

            def copy_keys_values(b):
                u = b.slot(2)
                wait_step(dve, att["kv_ps"], b)
                wait_step(dve, att["o_ps"], b.after(-2))
                nc.vector.tensor_tensor(k_first[:, u, :], bank5[:, 0:D], const["key_decay"], ALU.mult)
                for c in range(PAIR):
                    last = nc.vector.tensor_copy(v_diagonal(u, c), bank5[:, D * (1 + c):D * (2 + c)]
                                                 .rearrange("p (h e) -> p h e", h=HEADS))
                last.then_inc(att["kv_ready"], 1)

            def split_queries_keys(b):
                u = b.slot(2)
                q_ps, k_ps = bank4[:, 0:SEQ_LEN], bank4[:, SEQ_LEN:2 * SEQ_LEN]
                wait_step(dve, att["qk_ps"], b)
                wait_step(dve, att["q_high_ready"], b.after(-1), 2)
                nc.vector.tensor_copy(q_t_high[:, :], q_ps).then_inc(att["q_t_high_ready"], 1)
                wait_step(dve, SCORES_PS[1], b.after(-2))
                nc.vector.tensor_copy(k_high[:, u, :], k_ps).then_inc(att["k_high_ready"], 1)
                wait_step(dve, att["q_t_high_ready"], b)
                nc.vector.tensor_tensor(q_t_low[:, u, :], q_ps, q_t_high[:, :].bitcast(FP32), ALU.subtract)\
                  .then_inc(att["q_t_low_ready"], 1)
                wait_step(dve, att["k_high_ready"], b)
                nc.vector.tensor_tensor(k_low[:, u, :], k_ps, k_high[:, u, :].bitcast(FP32), ALU.subtract)\
                  .then_inc(att["k_ready"], 1)
                nc.vector.tensor_tensor(q_later[:, u, :], bank4[:, TILE:SEQ_LEN], const["query_decay"], ALU.mult)\
                  .then_inc(att["q_later_ready"], 1)

            def mask_state(b):
                wait_step(dve, att["state_ps"], b)
                nc.vector.tensor_tensor(state[:, b.slot(2), :], bank5[:, 3 * D:4 * D], const["same_head"], ALU.mult)\
                  .then_inc(att["state_ready"], 1)

            def add_projection(b):
                wait_step(dve, att["proj_ps"], b)
                nc.vector.tensor_tensor(x_pair(b), x_pair(b), bank7[:, SEQ_LEN:2 * SEQ_LEN], ALU.add)\
                  .then_inc(att["x_ready"], 1)

            def middle(s):
                if s.within(PAIRS):
                    weigh_scores(s, 1)
                if s.after(-1).within(PAIRS):
                    scale_mean(prep[1], s.after(-1), 1)
                if s.after(1).within(PAIRS):
                    split_queries_keys(s.after(1))
                    copy_keys_values(s.after(1))
                if s.after(2).within(PAIRS):
                    add_pick(0, 0, s.after(2))
                    add_pick(0, 1, s.after(2))
                    wait_step(dve, comb[0]["added"], s.after(2), PAIR)
                    take_stats(att, s.after(2), 0)
                    take_moments(att, s.after(2), 0)
                    invert_variance(att, s.after(2), 0)
                if s.after(2).within(PAIRS):
                    scale_mean(att, s.after(2), 0)
                if s.after(1).within(PAIRS):
                    mask_state(s.after(1))
                if s.after(-2).within(PAIRS):
                    add_router_bias(prep[1], s.after(-2), bank6[:, 0:SEQ_LEN])
                if s.after(1).within(PAIRS):
                    weigh_scores(s.after(1), 0)
                if s.within(PAIRS):
                    add_projection(s)
                    wait_step(dve, att["x_ready"], s)
                    take_stats(prep[1], s, 1)
                    take_moments(prep[1], s, 1)
                    invert_variance(prep[1], s, 1)

            run_steps(dve, PAIRS, 4, 2, 2, first_prep)
            dve.wait_ge(prep[0]["logits_ready"], PAIRS)
            dve.wait_ge(consts_ready, 1)
            route_rows(0)
            dve.wait_ge(route[0]["experts_ready"], 1)
            dve.wait_ge(weights_loaded, 16 * WEIGHT_LOADS)
            dve.wait_ge(bias1_ps, 1)
            nc.vector.tensor_copy(w1[:, :].rearrange("p (e f) -> p e f", e=EXPERTS)[:, :, FF:EXPERT_STEP],
                                  bank6[:, 0:EXPERTS * FF_CHUNKS].rearrange("p (e c) -> p e c", e=EXPERTS))\
              .then_inc(bias1_ready, 1)
            dve.wait_ge(bias1_ready, 1)
            run_experts(0)
            dve.wait_ge(v_zeroed, 1)
            run_steps(dve, PAIRS, 4, 2, 2, middle)
            dve.wait_ge(prep[1]["logits_ready"], PAIRS)
            route_rows(1)
            dve.wait_ge(route[1]["experts_ready"], 1)
            run_experts(1)
            for b in range(-1, PAIRS):
                last_adds(Step(b))

        @block.tensor
        def _(pe):
            identity = const["identity"]

            def transpose_norm(s, b, which, ps):
                wait_step(pe, s["norm_ready"], b)
                for t in range(PAIR):
                    last = nc.tensor.transpose(ps[:, t * TILE:(t + 1) * TILE],
                                               norm_slot(s, which, b)[:, t * D:(t + 1) * D], identity)
                last.then_inc(s["norm_t_ps"], 1)

            def router(s, b, ps):
                wait_step(pe, s["norm_t_ready"], b)
                for t in range(PAIR):
                    last = nc.tensor.matmul(ps[:, t * TILE:(t + 1) * TILE],
                                            norm_t[:, 1, b.slot(2), t * TILE:(t + 1) * TILE], w_router[:, :],
                                            start=True, stop=True)
                last.then_inc(s["logits_ps"], 1)

            def first_prep(s):
                b = s.after(1)
                if b.within(PAIRS):
                    transpose_norm(prep[0], b, 1, (bank6, bank7)[b.slot(2)][:, 0:SEQ_LEN])
                if s.within(PAIRS):
                    wait_step(pe, prep[0]["logits_ready"], s.after(-4))
                    router(prep[0], s, ps_logits[s.slot(4)])

            def route_rows(f):
                r = route[f]
                pe.wait_ge(r["picked"], 1)
                flat = picked_bf[:, :, :].rearrange("p t e -> p (t e)")
                nc.tensor.matmul(bank4[:, 0:256], before_bf[:, :], flat, start=True, stop=True)
                nc.tensor.matmul(bank4[:, 256:512], ones_bf[:, :], flat, start=True, stop=True)\
                  .then_inc(r["ranks_ps"], 1)

                def table_group(g):
                    u = g.slot(2)
                    wait_step(pe, r["low_ready"], g)
                    wait_step(pe, r["column_ready"], g)
                    wait_step(pe, r["base_ready"], g)
                    for i in range(HOT):
                        last = nc.tensor.matmul(bank5[:, 0:2 * SLOT_TILES], low_hot[:, u, i, :],
                                                high_value[:, u, i, :, :],
                                                start=g.turn is None and g.c == 0 and i == 0,
                                                stop=g.turn is None and g.c == PICKS // HOT - 1 and i == HOT - 1)
                    last.then_inc(r["table_ps"], 1)

                run_steps(pe, PICKS // HOT, 2, 0, 0, table_group, tail=2)

            offsets = {}

            def load_offsets(first, count):
                _, values = nc.values_load_multi_w_load_instructions(
                    expert_offset[0:1, bass.ds(first.n, count)], engines=[mybir.EngineType.PE], min_val=0,
                    max_val=(EXPERTS - 1) * EXPERT_STEP,
                    skip_runtime_bounds_check_because="a sum of EXPERTS - 1 comparisons times EXPERT_STEP")
                for i in range(count):
                    offsets[first.turn is None, first.c + i] = values[i]

            def offset(j):
                key = (j.turn is None, j.c)
                if key not in offsets:
                    load_offsets(j, 1)
                return offsets[key]

            def transpose_got(f, j):
                wait_slot(pe, gathered[f], j)
                wait_step(pe, expert[f]["got_t_ready"], j.after(-2))
                nc.tensor.transpose(ps_got_t[j.slot(2)], got[:, j.slot(4), :], identity)\
                  .then_inc(expert[f]["got_t_ps"], 1)

            def first_product(f, j):
                u = j.slot(2)
                wait_step(pe, expert[f]["got_t_ready"], j)
                wait_step(pe, expert[f]["w1_copied"], j)
                wait_step(pe, expert[f]["hidden_t_ready"], j.after(-2))
                for c in range(FF_CHUNKS):
                    last = nc.tensor.matmul(ps_hidden_t[u][:, c * TILE:(c + 1) * TILE],
                                            w1_now[:, u, c * TILE:(c + 1) * TILE], got_t[:, u, :],
                                            start=True, stop=True)
                last.then_inc(expert[f]["hidden_t_ps"], 1)

            def second_product(f, j):
                at, u = offset(j), j.slot(2)
                wait_step(pe, expert[f]["hidden_t_ready"], j)
                wait_step(pe, expert[f]["result_ready"], j.after(-2))
                for c in range(FF_CHUNKS):
                    last = nc.tensor.matmul(ps_result[u], hidden_t[:, u, c * TILE:(c + 1) * TILE],
                                            w2[:, bass.ds(at + c * D, D)], start=c == 0, stop=c == FF_CHUNKS - 1)
                last.then_inc(expert[f]["result_ps"], 1)

            def expert_step(f, s):
                if s.after(1).within(SLOT_TILES):
                    first_product(f, s.after(1))
                if s.within(SLOT_TILES):
                    second_product(f, s)
                if s.after(3).within(SLOT_TILES):
                    transpose_got(f, s.after(3))

            def run_experts(f):
                pe.wait_ge(route[f]["experts_ready"], 1)
                offsets.clear()
                run_steps(pe, SLOT_TILES, 4, 0, 3, lambda s: expert_step(f, s),
                          group=lambda first: load_offsets(first, 4))

            def project(b):
                u = b.slot(2)
                wait_step(pe, att["norm_t_ready"], b)
                wait_step(pe, att["state_ready"], b.after(-1))
                xt = norm_t[:, 0, u, :]
                nc.tensor.matmul(bank4[:, 0:SEQ_LEN], w_q[:, :], xt, start=True, stop=True)
                nc.tensor.matmul(bank4[:, SEQ_LEN:2 * SEQ_LEN], w_kv[:, 0:D], xt, start=True, stop=True)\
                  .then_inc(att["qk_ps"], 1)
                nc.tensor.matmul(bank5[:, 0:2 * D], xt[:, 0:TILE], w_kv[:, :], start=True, stop=True)
                nc.tensor.matmul(bank5[:, 2 * D:3 * D], xt[:, TILE:SEQ_LEN], w_kv[:, D:2 * D], start=True, stop=True)\
                  .then_inc(att["kv_ps"], 1)

            def make_state(b):
                u = b.slot(2)
                wait_step(pe, att["kv_ready"], b)
                nc.tensor.matmul(bank5[:, 3 * D:4 * D], k_first[:, u, :], v_diagonal(u, 0), start=True, stop=True)\
                  .then_inc(att["state_ps"], 1)

            def score(b, c, g):
                u = b.slot(2)
                pe.wait_ge(att["q_high_ready"], b.n * 2 + g + 1)
                if g == 0:
                    wait_step(pe, att["k_ready"], b)
                    pe.wait_ge(att["q_low_ready"], b.n * PAIR + c + 1)
                    wait_step(pe, WEIGHTS_READY[c], b.after(-1))
                keys, heads = slice(c * TILE, (c + 1) * TILE), slice(g * 4, (g + 1) * 4)
                parts = ((k_high, q_high), (k_low, q_high), (k_high, q_low))
                for n, (k, q) in enumerate(parts):
                    last = nc.tensor.matmul(ps_scores[c][:, g * 512:(g + 1) * 512], k[:, u, keys],
                                            q[:, u, heads, keys], start=n == 0, stop=n == len(parts) - 1)
                if g == 1:
                    last.then_inc(SCORES_PS[c], 1)

            def mix_values(b):
                u = b.slot(2)
                wait_step(pe, att["x_ready"], b.after(-1))
                for c in range(PAIR):
                    wait_step(pe, WEIGHTS_READY[c], b)
                    if c:
                        wait_step(pe, att["state_ready"], b)
                        wait_step(pe, att["q_later_ready"], b)
                        nc.tensor.matmul(bank7[:, TILE:SEQ_LEN], state[:, u, :], q_later[:, u, :],
                                         start=True, stop=False)
                    for h in range(HEADS):
                        last = nc.tensor.matmul(bank7[:, c * TILE:(c + 1) * TILE],
                                                v_blocks[:, u, c, h * TILE:(h + 1) * TILE],
                                                weights[:, c, h * TILE:(h + 1) * TILE],
                                                start=c == 0 and h == 0, stop=h == HEADS - 1)
                last.then_inc(att["o_ps"], 1)

            def project_out(b):
                wait_step(pe, att["o_ready"], b)
                for c in range(PAIR):
                    last = nc.tensor.matmul(bank7[:, SEQ_LEN + c * D:SEQ_LEN + (c + 1) * D],
                                            o_t[:, c * TILE:(c + 1) * TILE], w_o[:, :], start=True, stop=True)
                last.then_inc(att["proj_ps"], 1)

            def middle(s):
                if s.after(1).within(PAIRS):
                    project(s.after(1))
                if s.within(PAIRS):
                    mix_values(s)
                if s.after(1).within(PAIRS):
                    make_state(s.after(1))
                if s.after(-2).within(PAIRS):
                    router(prep[1], s.after(-2), bank6[:, 0:SEQ_LEN])
                if s.after(1).within(PAIRS):
                    score(s.after(1), 0, 0)
                    score(s.after(1), 0, 1)
                if s.within(PAIRS):
                    project_out(s)
                if s.after(1).within(PAIRS):
                    score(s.after(1), 1, 0)
                wait_step(pe, prep[1]["logits_ready"], s.after(-2))
                if s.after(-1).within(PAIRS):
                    transpose_norm(prep[1], s.after(-1), 1, bank6[:, SEQ_LEN:2 * SEQ_LEN])
                if s.after(2).within(PAIRS):
                    transpose_norm(att, s.after(2), 0, bank6[:, 0:SEQ_LEN])
                if s.after(1).within(PAIRS):
                    score(s.after(1), 1, 1)

            pe.wait_ge(consts_loaded, 16)
            pe.wait_ge(router_loaded, 16)
            pe.wait_ge(router_zeroed, 1)
            run_steps(pe, PAIRS, 4, 0, 1, first_prep)
            route_rows(0)
            pe.wait_ge(weights_loaded, 16 * WEIGHT_LOADS)
            pe.wait_ge(prep[0]["logits_ready"], PAIRS)
            nc.tensor.transpose(bank6[:, 0:EXPERTS * FF_CHUNKS], bias1_rows[:, :],
                                identity[0:EXPERTS * FF_CHUNKS, 0:EXPERTS * FF_CHUNKS]).then_inc(bias1_ps, 1)
            run_experts(0)
            pe.wait_ge(v_zeroed, 1)
            run_steps(pe, PAIRS, 2, 2, 2, middle)
            route_rows(1)
            run_experts(1)


def shape_constants():
    import numpy as np

    i = np.arange(TILE, dtype=np.float64)
    head = np.arange(D) // HEAD_DIM
    gamma = 1.0 - np.exp2(-5.0 - np.arange(HEADS, dtype=np.float64))
    scale = float(HEAD_DIM) ** -0.5
    parts = {
        "identity": np.eye(TILE),
        "same_head": head[:, None] == head[None, :],
        "query_decay": scale * gamma[head][:, None] ** (i[None, :] + 1),
        "key_decay": gamma[head][None, :] ** (TILE - 1 - i[:, None]),
        "before": i[:, None] < i[None, :],
        "column": np.broadcast_to(i[None, :], (TILE, TILE)),
        "head_rows": head[:, None] == np.arange(HEADS)[None, :],
        "low_first": np.broadcast_to((EXPERTS - np.arange(EXPERTS))[None, :], (TILE, EXPERTS)),
        "pick_base": (i[:, None] + 1) * PICKS,
    }
    table = np.zeros((TILE, CONST_WIDTH), np.float32)
    for name, (a, b) in CONST_COLUMNS.items():
        table[:, a:b] = parts[name]
    distance = i[None, None, :] - i[:, None, None]
    decay = np.where(distance >= 0, scale * gamma[None, :, None] ** np.maximum(distance, 0), 0.0)
    return table, decay.reshape(TILE, HEADS * TILE).astype(np.float32)


def kernel(L0_attn_hidden_states, L0_attn_rel_pos, L0_attn_Wq, L0_attn_Wk, L0_attn_Wv, L0_attn_Wo,
           L0_ffn_router_w, L0_ffn_router_b, L0_ffn_W1, L0_ffn_b1, L0_ffn_W2, L0_ffn_b2):
    import numpy as np
    import concourse.bacc as bacc
    from concourse.bass_utils import run_bass_kernel_spmd

    table, decay = shape_constants()
    arrays = {
        "hidden_states": L0_attn_hidden_states, "router_w": L0_ffn_router_w, "router_b": L0_ffn_router_b,
        "W1": L0_ffn_W1, "b1": L0_ffn_b1, "W2": L0_ffn_W2, "b2": L0_ffn_b2,
        "Wq": L0_attn_Wq, "Wk": L0_attn_Wk, "Wv": L0_attn_Wv, "Wo": L0_attn_Wo,
        "consts": table, "score_decay": decay,
    }
    arrays = {f"in_{n}": np.ascontiguousarray(a) for n, a in arrays.items()}
    nc = bacc.Bacc("TRN2", target_bir_lowering=False, num_devices=1)
    ins = [nc.dram_tensor(n, a.shape, mybir.dt.from_np(a.dtype), kind="ExternalInput").ap()
           for n, a in arrays.items()]
    out = nc.dram_tensor("out_rows", (SEQS, SEQ_LEN, D), FP32, kind="ExternalOutput").ap()
    build(nc, *ins, out)
    return run_bass_kernel_spmd(nc, [arrays], core_ids=[0]).results[0]["out_rows"]
```
